# Optimizing a Trainium2 kernel written in Bass

```python
import numpy as np
import jax
import jax.numpy as jnp

def _softmax(x, axis=-1):
    return jax.nn.softmax(x, axis=axis)

def _gelu(x):
    return jax.nn.gelu(x, approximate=True)

def _silu(x):
    return jax.nn.silu(x)

def _sigmoid(x):
    return jax.nn.sigmoid(x)

def _layernorm(x, axis=-1, eps=1e-05):
    m = jnp.mean(x, axis=axis, keepdims=True)
    v = jnp.var(x, axis=axis, keepdims=True)
    return (x - m) / jnp.sqrt(v + eps)

def _scatter_add(tgt, idx, src, axis=0):
    return tgt.at[idx].add(src)

def _segment_sum(src, seg, n):
    return jax.ops.segment_sum(src, seg, n)
kernel_name = 'mk_flamingo_gated_d1_seqx_r4_29505f'

def setup_inputs(seed: int=0):
    np.random.seed(seed)
    _w = jnp.asarray

    def _rec_inputs():
        import jax
        import jax.numpy as jnp
        _rk = jax.random.key(seed)
        x = 7.22e-05 + 1 * jax.random.normal(jax.random.fold_in(_rk, 1), (8, 256, 512), jnp.float32)
        _lenS = 256 - jax.random.randint(jax.random.fold_in(_rk, 7), (8,), 0, max(1, 256 // 4) + 1, jnp.int32)
        _lenS2 = 256 - jax.random.randint(jax.random.fold_in(_rk, 8), (8,), 0, max(1, 256 // 4) + 1, jnp.int32)
        _ctx_2048P = jax.random.normal(jax.random.fold_in(_rk, 11), (8, 16, 512), jnp.float32)
        _ctx_2048c = jax.random.dirichlet(jax.random.fold_in(_rk, 511), 0.3 * jnp.ones((16,), jnp.float32), (8, 256))
        _ctx_2048t = jnp.einsum('bsk,bkd->bsd', _ctx_2048c, _ctx_2048P)
        _ctx_2048t = _ctx_2048t * jax.lax.rsqrt(jnp.mean(jnp.square(_ctx_2048t)) + 1e-12) * 0.953939
        ctx_2048 = 4.13588e-05 + 0.999923 * (_ctx_2048t + 0.3 * jax.random.normal(jax.random.fold_in(_rk, 611), (8, 256, 512), jnp.float32))
        _g = jax.random.normal(jax.random.fold_in(_rk, 9001), (2, 1), jnp.float32)
        _g = jnp.sign(_g) * jnp.maximum(jnp.abs(_g), 1.0) + (_g == 0) * 1.0
        g_xattn = _g[0]
        g_ffn = _g[1]
        return (x, ctx_2048, g_xattn, g_ffn)
    x, ctx_2048, g_xattn, g_ffn = _rec_inputs()

    def _L0_xattn_setup():
        import jax, jax.numpy as jnp
        import numpy as np
        N_HEADS = 16
        K_CH = 256 // N_HEADS
        SCALE = 1.0 / np.sqrt(K_CH)
        key = jax.random.key(seed)
        ks = jax.random.split(key, 10)
        B, C, T = (4, 256, 512)
        Cout = 256
        xavier = lambda k, o, i: jax.random.uniform(k, (o, i), jnp.float32, -1.0, 1.0) * np.sqrt(6.0 / (o + i))
        return {'x': jax.random.normal(ks[0], (B, C, T), jnp.float32), 'c': jax.random.normal(ks[1], (B, C, T), jnp.float32), 'Wq': xavier(ks[2], C, C), 'bq': jnp.zeros((C,), jnp.float32), 'Wk': xavier(ks[3], C, C), 'bk': jnp.zeros((C,), jnp.float32), 'Wv': xavier(ks[4], C, C), 'bv': jnp.zeros((C,), jnp.float32), 'Wo': xavier(ks[5], Cout, C), 'bo': jnp.zeros((Cout,), jnp.float32)}
    _L0_xattn_all = _L0_xattn_setup()
    _L0_xattn_in = {k: v for k, v in _L0_xattn_all.items() if k in ('Wq', 'bq', 'Wk', 'bk', 'Wv', 'bv', 'Wo', 'bo')}
    del _L0_xattn_all

    def _L0_ffn_setup():
        import jax, jax.numpy as jnp
        import numpy as np
        NUM_EXPERTS = 12
        TOP_K = 2
        FFN_DIM = 320
        HIDDEN = 512
        key = jax.random.key(seed)
        k0, k1, k2, k3, k4 = jax.random.split(key, 5)
        B, S, H, F, E = (4, 256, HIDDEN, FFN_DIM, NUM_EXPERTS)
        hidden_states = jax.random.normal(k0, (B, S, H), dtype=jnp.float32)
        gate_w = jax.random.normal(k1, (E, H), dtype=jnp.float32) * 0.02
        w1 = jax.random.normal(k2, (E, F, H), dtype=jnp.float32) * 0.02
        w2 = jax.random.normal(k3, (E, H, F), dtype=jnp.float32) * 0.02
        w3 = jax.random.normal(k4, (E, F, H), dtype=jnp.float32) * 0.02
        return {'hidden_states': hidden_states, 'gate_w': gate_w, 'w1': w1, 'w2': w2, 'w3': w3}
    _L0_ffn_all = _L0_ffn_setup()
    _L0_ffn_in = {k: v for k, v in _L0_ffn_all.items() if k in ('gate_w', 'w1', 'w2', 'w3')}
    del _L0_ffn_all
    return {'x': x, 'ctx_2048': ctx_2048, 'g_xattn': g_xattn, 'g_ffn': g_ffn, 'L0_xattn_Wq': _L0_xattn_in['Wq'], 'L0_xattn_bq': _L0_xattn_in['bq'], 'L0_xattn_Wk': _L0_xattn_in['Wk'], 'L0_xattn_bk': _L0_xattn_in['bk'], 'L0_xattn_Wv': _L0_xattn_in['Wv'], 'L0_xattn_bv': _L0_xattn_in['bv'], 'L0_xattn_Wo': _L0_xattn_in['Wo'], 'L0_xattn_bo': _L0_xattn_in['bo'], 'L0_ffn_gate_w': _L0_ffn_in['gate_w'], 'L0_ffn_w1': _L0_ffn_in['w1'], 'L0_ffn_w2': _L0_ffn_in['w2'], 'L0_ffn_w3': _L0_ffn_in['w3']}

def reference(x, ctx_2048, g_xattn, g_ffn, L0_xattn_Wq, L0_xattn_bq, L0_xattn_Wk, L0_xattn_bk, L0_xattn_Wv, L0_xattn_bv, L0_xattn_Wo, L0_xattn_bo, L0_ffn_gate_w, L0_ffn_w1, L0_ffn_w2, L0_ffn_w3):
    import jax
    import jax.numpy as jnp

    def _L0_xattn_ref(x, c, Wq, bq, Wk, bk, Wv, bv, Wo, bo):
        import jax, jax.numpy as jnp
        import numpy as np
        N_HEADS = 16
        K_CH = 256 // N_HEADS
        SCALE = 1.0 / np.sqrt(K_CH)
        B, C, T = x.shape
        H, K = (N_HEADS, K_CH)
        q = jnp.einsum('oc,bct->bot', Wq, x) + bq[None, :, None]
        k = jnp.einsum('oc,bct->bot', Wk, c) + bk[None, :, None]
        v = jnp.einsum('oc,bct->bot', Wv, c) + bv[None, :, None]
        q = q.reshape(B, H, K, T)
        k = k.reshape(B, H, K, -1)
        v = v.reshape(B, H, K, -1)
        scores = jnp.einsum('bhkt,bhks->bhts', q, k) * SCALE
        p = jax.nn.softmax(scores, axis=-1)
        out = jnp.einsum('bhts,bhks->bhkt', p, v)
        out = out.reshape(B, H * K, T)
        return jnp.einsum('oc,bct->bot', Wo, out) + bo[None, :, None]

    def _L0_ffn_ref(hidden_states, gate_w, w1, w2, w3):
        import jax, jax.numpy as jnp
        import numpy as np
        NUM_EXPERTS = 12
        TOP_K = 2
        FFN_DIM = 320
        HIDDEN = 512
        B, S, H = hidden_states.shape
        x = hidden_states.reshape(-1, H)
        T = x.shape[0]
        logits = x @ gate_w.T
        probs = jax.nn.softmax(logits, axis=-1)
        top_w, top_i = jax.lax.top_k(probs, TOP_K)
        top_w = top_w / jnp.sum(top_w, axis=-1, keepdims=True)
        cw = jnp.zeros((T, NUM_EXPERTS), dtype=x.dtype)
        cw = cw.at[jnp.arange(T)[:, None], top_i].add(top_w)
        out = jnp.zeros_like(x)
        for e in range(NUM_EXPERTS):
            h = jax.nn.silu(x @ w1[e].T) * (x @ w3[e].T)
            out = out + h @ w2[e].T * cw[:, e:e + 1]
        return out.reshape(B, S, H)
    x = x + jnp.tanh(g_xattn[0]) * _L0_xattn_ref(_layernorm(x, axis=-1), ctx_2048, L0_xattn_Wq, L0_xattn_bq, L0_xattn_Wk, L0_xattn_bk, L0_xattn_Wv, L0_xattn_bv, L0_xattn_Wo, L0_xattn_bo)
    x = x + jnp.tanh(g_ffn[0]) * _L0_ffn_ref(_layernorm(x, axis=-1), L0_ffn_gate_w, L0_ffn_w1, L0_ffn_w2, L0_ffn_w3)
    return x

_drawn_inputs = setup_inputs


def setup_inputs(seed=0):
    import zlib

    import numpy as np

    out = dict(_drawn_inputs(seed))
    spreads = {'L0_xattn_bq': (0.0, 0.294),
     'L0_xattn_bk': (0.0, 0.8),
     'L0_xattn_bv': (0.0, 0.1),
     'L0_xattn_bo': (0.0, 0.1)}
    factors = {}
    for name, (base, spread) in spreads.items():
        noise = np.random.default_rng([zlib.crc32(name.encode()), seed]).standard_normal(out[name].shape)
        drawn = base * np.exp(spread * noise) if base else spread * noise
        out[name] = jnp.asarray(drawn.astype(out[name].dtype))
    for name, factor in factors.items():
        out[name] = (out[name] * factor).astype(out[name].dtype)
    return out
```

```python
from contextlib import ExitStack

import concourse.bass as bass
from concourse import mybir

ALU = mybir.AluOpType
ACT = mybir.ActivationFunctionType
AX_X = mybir.AxisListType.X
F32 = mybir.dt.float32
F16 = mybir.dt.float16
I32 = mybir.dt.int32
U32 = mybir.dt.uint32
U16 = mybir.dt.uint16

P = 128
EPS = 1e-5


class At:

    def __init__(self, i, mul, add):
        self.i, self.mul, self.add = i, mul, add

    def value(self, k=1, c=0):
        if self.i is None:
            return k * self.add + c
        return self.i * (k * self.mul) + (k * self.add + c)

    def before(self, n):
        return At(self.i, self.mul, self.add - n)


def wait(eng, sem, at, k, c=0, alone=None):
    if at.i is None and k * at.add + c <= 0:
        return
    assert k * at.add + c > 0, "a wait against nothing in a loop's first round"
    value = at.value(k, c)
    if alone is not None and at.i is not None:
        value = eng.to_reg(value)
        eng.wait_ge(alone, 1)
    eng.wait_ge(sem, value)


class Signals:

    def __init__(self, sem):
        self.xc = sem("xc")
        self.bst, self.mv, self.veps, self.rstd, self.xn = sem("bst"), sem("mv"), sem("veps"), sem("rstd"), sem("xn")
        self.bst2, self.mv2, self.veps2, self.rstd2, self.xn2 = (
            sem("bst2"), sem("mv2"), sem("veps2"), sem("rstd2"), sem("xn2"))
        self.a_full, self.a_free = sem("a_full"), sem("a_free")
        self.c_full = sem("c_full")
        self.c_free = sem("c_free")
        self.qh, self.ql, self.kh, self.kl = sem("qh"), sem("ql"), sem("kh"), sem("kl")
        self.qkst = sem("qkst")
        self.qk = sem("qk")
        self.full = sem("full")
        self.exp = sem("exp")
        self.pv = sem("pv")
        self.os = sem("os")
        self.zl = sem("zl")
        self.rz = sem("rz")
        self.zst = sem("zst")
        self.oz = sem("oz")
        self.on = sem("on")
        self.xb = sem("xb")
        self.xnst = sem("xnst")
        self.ok = sem("ok")
        self.raw = sem("raw")
        self.top = sem("top")
        self.turned = sem("turned")
        self.shift = sem("shift")
        self.shst = sem("shst")
        self.shld = sem("shld")


def flamingo_kernel(nc, x, ctx_in, g_xattn, g_ffn, WqT, bq, WkT, bk, WvT, bv, WoT, bo, gateT, w13T, w2T, out):
    B, C, T = x.shape
    H, DK = 16, C // 16
    CT, TT = C // P, T // P
    NE = gateT.shape[1]
    F = w2T.shape[1]
    FT = -(-F // P)
    FL = F - (FT - 1) * P
    TOP = 2
    TOK = B * C
    NT = TOK // P
    TILES = (TOP * TOK + NE * (P - 1)) // P
    SCALE = DK ** -0.5
    ZW = H * T // P
    G = H // 2
    SHIFT = 64.0
    PARTS = 3
    GROUPS, GH = H // 4, 4
    RING = 4
    UM = H * TT // 2
    Z_LEAST, Z_MOST = 1e-20, 1e30
    EB = 4
    WCOL = TT * 2 * F + FT * T

    q_dram = nc.dram_tensor("q_parts", [2, C, T], F16).ap()
    k_dram = nc.dram_tensor("k_parts", [2, C, T], F16).ap()
    z_dram = nc.dram_tensor("inverse_sums", [GH, GROUPS, T], F32).ap()
    shift_dram = nc.dram_tensor("shift_rows", [H, T], F16).ap()
    xn_dram = nc.dram_tensor("tokens_normed", [TOK, T], F32).ap()
    y_dram = nc.dram_tensor("slot_outputs", [TILES * P, T], F32).ap()

    x_v = x.rearrange("b (m p) t -> b p m t", p=P)
    c_v = ctx_in.rearrange("b (m p) t -> b p m t", p=P)
    out_v = out.rearrange("b (m p) t -> (b m) p t", p=P)

    top = ExitStack()
    with top:
        def sb(name, shape, dt=F32, stack=top):
            return stack.enter_context(nc.sbuf_tensor(name, shape, dt))

        def sem(name):
            return top.enter_context(nc.semaphore(name))

        res = sb("residual", [P, NT * T])
        ident = sb("ident", [P, P])
        ones = sb("ones", [P, P])
        below = sb("below", [P, P])
        gate = sb("gate", [P, TT, NE])
        logits = sb("logits", [P, NT * NE])
        rows = sb("rows", [1, 2 * C + 2])
        cols = sb("cols", [P, 4 * CT + 4])
        ok = sb("ok", [P, ZW])
        ok_min = sb("ok_min", [P, 1])
        bad = sb("bad", [P, 1], U16)
        maxima = sb("maxima", [P, H * TT])
        shift_t = sb("shift_t", [H * TT, P], F16)
        neg_half = sb("neg_half", [P, CT])

        att = ExitStack()
        ctx_sb = [sb(f"ctx{i}", [P, CT, T], F32, att) for i in range(2)]
        xn = sb("xn", [P, CT, T], F32, att)
        qf = sb("qf", [P, CT, T], F32, att)
        kf = sb("kf", [P, CT, T], F32, att)
        qs = sb("qs", [P, 2, CT, T], F16, att)
        ks = sb("ks", [P, 2, CT, T], F16, att)
        Q = [sb(f"Q{i}", [P, G, T], F16, att) for i in range(2)]
        K = [sb(f"K{i}", [P, G, T], F16, att) for i in range(2)]
        V = [sb(f"V{i}", [P, TT, H, 2 * DK], F32, att) for i in range(2)]
        prob = sb("prob", [P, RING, 2 * T], F32, att)
        osum = [sb(f"osum{i}", [P, GROUPS, T], F32, att) for i in range(2)]
        oc = sb("oc", [P, CT, T], F32, att)
        zc = sb("zc", [P, CT, T], F32, att)
        zl = sb("zl", [P, ZW], F32, att)
        zr = sb("zr", [P, ZW], F32, att)
        on = sb("on", [P, CT, T], F32, att)
        xn2 = sb("xn2", [P, CT, T], F32, att)
        xT2 = sb("xT2", [P, CT, T], F32, att)
        wq = sb("wq", [P, CT, C], F32, att)
        wk = sb("wk", [P, CT, C], F32, att)
        wv = sb("wv", [P, CT, C], F32, att)
        wo = sb("wo", [P, CT, C], F32, att)
        bv_all = sb("bv_all", [P, C], F32, att)
        stats = sb("stats", [P, CT, 6], F32, att)
        mv = sb("mv", [P, CT, 2], F32, att)
        veps = sb("veps", [P, CT], F32, att)
        rstd = sb("rstd", [P, CT], F32, att)
        stats2 = sb("stats2", [P, CT, 6], F32, att)
        mv2 = sb("mv2", [P, CT, 2], F32, att)
        veps2 = sb("veps2", [P, CT], F32, att)
        rstd2 = sb("rstd2", [P, CT], F32, att)
        att.close()

        top8 = sb("top8", [P, NT, 8])
        idx8 = sb("idx8", [P, NT, 8], U32)
        idxf = sb("idxf", [P, TOP, NT])
        dl = sb("dl", [P, NT])
        el = sb("el", [P, NT])
        el1 = sb("el1", [P, NT])
        cw = sb("cw", [P, TOP, NT])
        cwg = sb("cwg", [P, TOP, NT])
        iota_i = sb("iota_i", [P, P], I32)
        iota_f = sb("iota_f", [P, P])
        tok_i = sb("tok_i", [P, TOP * NT], I32)
        tok_f = sb("tok_f", [P, TOP * NT])
        onehot = sb("onehot", [P, TOP, NT, NE])
        picks = sb("picks", [P, NT, NE])
        count_et = sb("count_et", [P, NE * NT])
        keep_et = sb("keep_et", [P, NE * NT])
        upto_et = sb("upto_et", [P, NE * NT])
        prev_et = sb("prev_et", [P, NE * NT])
        tot_f = sb("tot_f", [P, NE])
        tot_i = sb("tot_i", [P, NE], I32)
        ntl_i = sb("ntl_i", [P, NE], I32)
        ntl = sb("ntl", [P, NE])
        endt = sb("endt", [P, NE])
        startt = sb("startt", [P, NE])
        slot_e = sb("slot_e", [P, NT, NE])
        slot_m = sb("slot_m", [P, TOP, NT, NE])
        slot_f = sb("slot_f", [P, TOP * NT])
        slot_i = sb("slot_i", [P, TOP * NT], I32)
        til_i = sb("til_i", [P, TOP * NT], I32)
        row_i = sb("row_i", [P, TOP * NT], I32)
        til_f = sb("til_f", [P, TOP * NT])
        row_f = sb("row_f", [P, TOP * NT])
        row_hot = sb("row_hot", [P, TOP * NT, P], F16)
        til_hot = sb("til_hot", [P, TOP * NT, TILES], F16)
        til_tok = sb("til_tok", [P, TOP * NT, TILES], F16)
        slot_tok = sb("slot_tok", [P, TILES], U32)
        le = sb("le", [P, TILES, NE])
        et_f = sb("et_f", [P, TILES])
        et_i = sb("et_i", [P, TILES], I32)
        eb_i = sb("eb_i", [P, TILES], I32)
        eo_i = sb("eo_i", [P, TILES], I32)
        table = sb("table", [P, 2 * TILES + NE], U16)
        W = sb("W", [P, EB * WCOL])
        xg = [sb(f"xg{i}", [P, T]) for i in range(2)]
        xT = [sb(f"xT{i}", [P, TT, P]) for i in range(2)]
        act1 = [sb(f"act1_{i}", [P, F]) for i in range(2)]
        hh = [sb(f"hh{i}", [P, F]) for i in range(2)]
        hT = [sb(f"hT{i}", [P, FT, P]) for i in range(2)]
        yo = [sb(f"yo{i}", [P, T]) for i in range(2)]
        CB = 3
        y0 = [sb(f"y0_{i}", [P, T]) for i in range(CB)]
        y1 = [sb(f"y1_{i}", [P, T]) for i in range(CB)]
        o1 = [sb(f"o1_{i}", [P, T]) for i in range(CB)]
        o2 = [sb(f"o2_{i}", [P, T]) for i in range(CB)]

        S = [top.enter_context(nc.psum_tensor(f"S{i}", [P, 2 * T], F32)) for i in range(2)]
        O = [top.enter_context(nc.psum_tensor(f"O{i}", [P, T], F32)) for i in range(2)]
        MA = top.enter_context(nc.psum_tensor("MA", [P, T], F32))
        MC = top.enter_context(nc.psum_tensor("MC", [P, T], F32))
        h1_ps, h3_ps = S[0][:, 0:F], S[0][:, T:T + F]
        xt_ps, ht_ps = S[1][:, 0:T], S[1][:, T:2 * T]
        y_ps = O[0]

        bq_c, bk_c, bo_c = (cols[:, n * CT:(n + 1) * CT] for n in range(3))
        bog_c = cols[:, 3 * CT:4 * CT]
        tg_c = cols[:, 4 * CT:4 * CT + 2]
        bv_r = rows[:, 0:C]
        g_r = rows[:, 2 * C:2 * C + 2]

        fast = Signals(lambda name: sem("f_" + name))
        slow = Signals(lambda name: sem("g_" + name))
        s_okall = sem("s_okall")
        s_oksum = sem("s_oksum")
        s_bad = sem("s_bad")
        s_rows = sem("s_rows")
        s_done = sem("s_done")

        def both_runs(eng, attention):
            attention(eng, fast, False)
            eng.wait_ge(s_bad, 1)
            with eng.If(eng.value_load(bad[0:1, 0:1], min_val=0, max_val=1) > 0):
                attention(eng, slow, True)

        NCONST = 4 + 3 + 1 + 2 + 1
        s_const = sem("s_const")
        s_pool_c = sem("s_pool_c")
        s_init = sem("s_init")
        s_bias = sem("s_bias")
        s_tanh = sem("s_tanh")
        s_bog = sem("s_bog")
        s_vone = sem("s_vone")
        A_USES = {n: k for k, n in enumerate(("k0", "k1", "q0", "q1", "v0", "v1"))}
        C_USES = {n: k for k, n in enumerate(("o0", "o1", "t0", "t1", "lg"))}
        NA, NCU = len(A_USES), len(C_USES)
        EXTRA = {3: "k0", 4: "k1", 5: "q0", 6: "q1", 7: "v0", 8: "o0", 9: "o1", 10: "v1", 12: "t0", 13: "t1", 14: "lg"}
        ON_AT, XN2_AT = 5, 11
        VS = GROUPS * TT

        def slots(eng, slot):
            slot(eng, At(None, 0, 0), 0, True, False, False)
            slot(eng, At(None, 0, 1), 1, True, True, False)
            with eng.Fori(0, (B - 2) // 2) as i:
                slot(eng, At(i, 2, 2), 0, True, True, True)
                slot(eng, At(i, 2, 3), 1, True, True, True)
            slot(eng, At(None, 0, B), 0, False, True, True)
            slot(eng, At(None, 0, B + 1), 1, False, False, True)

        s_r = sem("s_r")
        s_wexp = sem("s_wexp")
        s_rank = sem("s_rank")
        s_tab = sem("s_tab")
        s_tok = sem("s_tok")
        s_table = sem("s_table")
        s_w = [sem(f"s_w{i}") for i in range(EB)]
        s_wr = sem("s_wr")
        s_xg = [sem(f"s_xg{i}") for i in range(2)]
        s_xt = sem("s_xt")
        s_xT = sem("s_xT")
        s_h = sem("s_h")
        s_silu = sem("s_silu")
        s_hh = sem("s_hh")
        s_ht = sem("s_ht")
        s_hT = sem("s_hT")
        s_y = sem("s_y")
        s_yo = sem("s_yo")
        s_yst = [sem(f"s_yst{i}") for i in range(2)]
        s_gy = [sem(f"s_gy{i}") for i in range(CB)]
        s_o1, s_o2 = sem("s_o1"), sem("s_o2")
        s_out = [sem(f"s_out{i}") for i in range(CB)]

        ranks, hots = [0], [0]

        block = top.enter_context(nc.Block())

        @block.sync
        def _(sp):
            for dst, src in ((wk, WkT), (wq, WqT), (wv, WvT), (wo, WoT)):
                sp.dma_start(dst[:, :, :], src.rearrange("(k p) n -> p k n", p=P)).then_inc(s_const, 16)
            for dst, src in ((bq_c, bq), (bk_c, bk), (bo_c, bo)):
                sp.dma_start(dst, src).then_inc(s_const, 16)
            sp.dma_start(bv_r, bv.rearrange("(a n) -> a n", a=1)).then_inc(s_const, 16)
            for n, g in enumerate((g_xattn, g_ffn)):
                sp.dma_start(g_r[:, n:n + 1], g.rearrange("(a n) -> a n", a=1)).then_inc(s_const, 16)
            sp.dma_start(gate[:, :, :], gateT.rearrange("(k p) n -> p k n", p=P)).then_inc(s_const, 16)

            def attention(sp, g, guard):
                sp.sem_inc(g.oz, 16)
                sp.sem_inc(g.xnst, 16)

                def load_batch(b, par):
                    sp.dma_start(res[:, bass.ds(b.value(CT * T), CT * T)].rearrange("p (m t) -> p m t", m=CT),
                                 x_v[bass.ds(b.value(), 1)].rearrange("b p m t -> p (b m) t")).then_inc(g.xc, 16)
                    sp.dma_start(ctx_sb[par][:, :, :],
                                 c_v[bass.ds(b.value(), 1)].rearrange("b p m t -> p (b m) t")).then_inc(g.xc, 16)

                def slot(sp, t, par, a, b_, c):
                    if b_ and guard:
                        bb = t.before(1)
                        wait(sp, g.shld, bb, 32, 0, s_bog)
                        wait(sp, g.shift, bb, 1, 1, s_bog)
                        sp.dma_start(shift_dram.rearrange("h (n p) -> (h n) p", p=P), shift_t[:, :])\
                            .then_inc(g.shst, 16)
                        wait(sp, g.shst, bb, 16, 16, s_bog)
                        for s in range(2):
                            row = 64 * s + PARTS * DK
                            sp.dma_start(Q[1 - par][row:row + 1, :, :],
                                         shift_dram.rearrange("(a g s) t -> s a g t", s=2, a=1)[s]).then_inc(g.shld, 16)
                    if a:
                        wait(sp, g.xc, t, 32, 0, s_bog)
                        wait(sp, g.a_free, t, NA, -NA)
                        load_batch(t, par)
                    if c:
                        bc = t.before(2)
                        wait(sp, g.os, bc, GROUPS, GROUPS, s_bog)
                        wait(sp, g.on, bc, 1, 1)
                        for j in range(GH):
                            sp.dma_start(zl[32 * j:32 * (j + 1), :], osum[par][2 * DK * j + DK:2 * DK * j + DK + 1, :, :])\
                                .then_inc(g.zl, 16)
                        for half in range(2):
                            for j in range(GH):
                                dst0 = 64 * half + DK * j
                                src = osum[par][2 * DK * j:2 * DK * j + DK, half::2, :]
                                sp.dma_start(oc[dst0:dst0 + DK, :, :], src).then_inc(g.oz, 16)
                        wait(sp, g.rz, bc, 1, 1)
                        sp.dma_start(z_dram.rearrange("j g t -> (j g t)").rearrange("(p n) -> p n", p=P), zr[:, :])\
                            .then_inc(g.zst, 16)
                        wait(sp, g.zst, bc, 16, 16)
                        for half in range(2):
                            for j in range(GH):
                                dst0 = 64 * half + DK * j
                                src = z_dram[j:j + 1, half::2, :].to_broadcast([DK, CT, T])
                                sp.dma_start(zc[dst0:dst0 + DK, :, :], src).then_inc(g.oz, 16)
                    if a:
                        wait(sp, g.qk, t, 16 * 4 * PARTS, 0, s_bog)
                        wait(sp, g.kl, t, 1, 1)
                        sp.dma_start(k_dram.rearrange("h (m p) t -> p h m t", p=P), ks[:, :, :, :]).then_inc(g.qkst, 16)
                        wait(sp, g.ql, t, 1, 1)
                        sp.dma_start(q_dram.rearrange("h (m p) t -> p h m t", p=P), qs[:, :, :, :]).then_inc(g.qkst, 16)
                        wait(sp, g.qkst, t, 32, 32, s_bog)
                        wait(sp, g.full, t, 2 * VS, -2 * VS)
                        sp.wait_ge(s_rows, 8)
                        for s in range(2):
                            for r, (qp, kp) in enumerate(((0, 0), (1, 0), (0, 1))):
                                for stack, dram, part in ((Q, q_dram, qp), (K, k_dram, kp)):
                                    src = dram[part].rearrange("(g s c) t -> s c g t", s=2, c=DK)[s]
                                    sp.dma_start(stack[par][64 * s + DK * r:64 * s + DK * (r + 1), :, :], src)\
                                        .then_inc(g.qk, 16)
                    if c:
                        bc = t.before(2)
                        wait(sp, g.xn2, bc, CT, CT, s_bog)
                        dst = xn_dram[bass.ds(bc.value(C), C)].rearrange("(m p) t -> p m t", p=P)
                        sp.dma_start(dst, xn2[:, :, :]).then_inc(g.xnst, 16)

                slots(sp, slot)
                sp.wait_ge(g.xnst, 16 * B + 16)

            both_runs(sp, attention)

            sp.wait_ge(s_done, 2)
            for e in range(NE):
                if e == EB:
                    sp.wait_ge(s_table, 1)
                if e >= EB:
                    end = sp.value_load(table[0:1, 2 * TILES + e - EB:2 * TILES + e - EB + 1], min_val=1, max_val=TILES + 1)
                    sp.wait_ge(s_y, end)
                w = W[:, (e % EB) * WCOL:(e % EB + 1) * WCOL]
                sp.dma_start(w[:, 0:TT * 2 * F].rearrange("p (k n) -> p k n", k=TT),
                             w13T[e].rearrange("(k p) n -> p k n", p=P)).then_inc(s_wr, 16)
                sp.dma_start(w[:, TT * 2 * F:TT * 2 * F + (FT - 1) * T].rearrange("p (k n) -> p k n", n=T),
                             w2T[e, 0:(FT - 1) * P].rearrange("(k p) n -> p k n", p=P)).then_inc(s_wr, 16)
                sp.dma_start(w[0:FL, TT * 2 * F + (FT - 1) * T:WCOL], w2T[e, (FT - 1) * P:F]).then_inc(s_wr, 16)
                sp.wait_ge(s_wr, 48 * (e + 1))

            for n in range(NT):
                sp.wait_ge(s_o2, n + 1)
                sp.dma_start(out_v[n], o2[n % CB][:, :]).then_inc(s_out[n % CB], 16)
            for m in range(CB):
                sp.wait_ge(s_out[m], 16 * len(range(m, NT, CB)))

        @block.gpsimd
        def _(pool):
            pool.memset(ident[:, :], 0.0).then_inc(s_pool_c, 1)
            pool.memset(ones[:, :], 1.0).then_inc(s_pool_c, 1)
            pool.memset(neg_half[:, :], -0.5).then_inc(s_pool_c, 1)
            pool.wait_ge(s_pool_c, 3)
            pool.affine_select(out=ident[:, :], in_=ident[:, :], compare_op=ALU.not_equal, fill=1.0, base=0,
                               pattern=[[-1, P]], channel_multiplier=1).then_inc(s_pool_c, 1)
            pool.affine_select(out=below[:, :], in_=ones[:, :], compare_op=ALU.is_gt, fill=0.0, base=0,
                               pattern=[[1, P]], channel_multiplier=-1).then_inc(s_pool_c, 1)
            for i in range(2):
                pool.memset(V[i][:, :, :, DK:2 * DK], 1.0).then_inc(s_vone, 1)

            def attention(pool, g, guard):
                def slot(pool, t, par, a, b_, c):
                    if a:
                        pool.wait_ge(s_pool_c, 5)
                        wait(pool, g.mv, t, CT, CT, s_pool_c)
                        pool.tensor_scalar(veps[:, :], mv[:, :, 1], EPS, None, ALU.add).then_inc(g.veps, 1)
                        wait(pool, g.veps, t, 1, 1)
                        pool.tensor_tensor(rstd[:, :], veps[:, :], neg_half[:, :], ALU.pow).then_inc(g.rstd, 1)
                        for f, parts, last, hi, lo in ((kf, ks, "k1", g.kh, g.kl), (qf, qs, "q1", g.qh, g.ql)):
                            wait(pool, g.qkst, t, 32, 0, s_pool_c)
                            wait(pool, g.a_free, t, NA, A_USES[last] + 1, s_pool_c)
                            pool.tensor_copy(parts[:, 0], f[:, :, :]).then_inc(hi, 1)
                            wait(pool, hi, t, 1, 1)
                            pool.tensor_tensor(parts[:, 1], f[:, :, :], parts[:, 0], ALU.subtract).then_inc(lo, 1)
                    if c:
                        bc = t.before(2)
                        wait(pool, g.mv2, bc, CT, CT, s_pool_c)
                        pool.tensor_scalar(veps2[:, :], mv2[:, :, 1], EPS, None, ALU.add).then_inc(g.veps2, 1)
                        wait(pool, g.veps2, bc, 1, 1)
                        pool.tensor_tensor(rstd2[:, :], veps2[:, :], neg_half[:, :], ALU.pow).then_inc(g.rstd2, 1)

                slots(pool, slot)

            both_runs(pool, attention)

            pool.wait_ge(s_done, 2)
            pool.iota(iota_i[:, :], pattern=[[1, P]], base=0, channel_multiplier=0).then_inc(s_pool_c, 1)
            pool.iota(tok_i[:, :], pattern=[[0, TOP], [P, NT]], base=0, channel_multiplier=1).then_inc(s_pool_c, 1)
            pool.memset(keep_et[:, :], 1.0).then_inc(s_pool_c, 1)
            pool.wait_ge(s_pool_c, 8)
            pool.tensor_copy(iota_f[:, :], iota_i[:, :]).then_inc(s_pool_c, 1)
            pool.tensor_copy(tok_f[:, :], tok_i[:, :]).then_inc(s_pool_c, 1)
            pool.memset(keep_et[:, ::NT], 0.0).then_inc(s_pool_c, 1)

            pool.wait_ge(s_tok, 1)
            for j in range(TILES):
                if j >= 2:
                    pool.wait_ge(s_xt, j - 1)
                pool.indirect_dma_start(out=xg[j % 2][:, :], out_offset=None, in_=xn_dram[:, :],
                                        in_offset=bass.IndirectOffsetOnAxis(ap=slot_tok[:, j:j + 1], axis=0))\
                    .then_inc(s_xg[j % 2], 16)

            for m in range(2):
                pool.wait_ge(s_yst[m], 16 * len(range(m, TILES, 2)))
            for n in range(NT):
                if n >= CB:
                    pool.wait_ge(s_o2, n - CB + 1)
                for k, y in enumerate((y0, y1)):
                    pool.indirect_dma_start(
                        out=y[n % CB][:, :], out_offset=None, in_=y_dram[:, :],
                        in_offset=bass.IndirectOffsetOnAxis(ap=slot_i[:, k * NT + n:k * NT + n + 1].bitcast(U32), axis=0))\
                        .then_inc(s_gy[n % CB], 16)

        @block.scalar
        def _(act):
            act.wait_ge(s_bias, 2)
            act.activation(tg_c, cols[:, 4 * CT + 2:4 * CT + 4], ACT.Tanh).then_inc(s_tanh, 1)

            for i in range(2):
                for r0 in (64 * s + 32 for s in range(2)):
                    one = ones[r0:r0 + 32, 0:1].to_broadcast([32, G * T])
                    for stack, factor in ((Q, 0.0), (K, SHIFT)):
                        act.activation(stack[i][r0:r0 + 32, :, :].rearrange("p g t -> p (g t)"), one, ACT.Copy,
                                       scale=factor).then_inc(s_rows, 1)

            def attention(act, g, guard):
                def slot(act, t, par, a, b_, c):
                    if not b_:
                        return
                    b = t.before(1)
                    for u in range(2 * VS):
                        wait(act, g.full, b, 2 * VS, u + 1)
                        wait(act, g.pv, b, VS, u // 2 - RING // 2 + 1)
                        act.activation(prob[:, u % RING, :], S[u % 2][:, :], ACT.Exp, scale=SCALE).then_inc(g.exp, 1)

                slots(act, slot)

            both_runs(act, attention)

            act.wait_ge(s_wexp, 1)
            act.activation(el[:, :], dl[:, :], ACT.Exp).then_inc(s_wexp, 1)

            def step(act, j, par, first):
                wait(act, s_h, j, 1, 1)
                if not first:
                    wait(act, s_hh, j, 1, -1)
                act.activation(act1[par][:, :], h1_ps, ACT.Silu).then_inc(s_silu, 1)

            def store(act, j, par):
                wait(act, s_y, j, 1, 2)
                if not (j.i is None and j.add < 2):
                    if par == 0:
                        act.wait_ge(s_yst[par], At(j.i, j.mul // 2, j.add // 2).value(16))
                    else:
                        act.wait_ge(s_yst[par], At(j.i, j.mul // 2, j.add // 2).value(16))
                act.activation(yo[par][:, :], y_ps[:, :], ACT.Copy).then_inc(s_yo, 1)
                wait(act, s_yo, j, 1, 1)
                act.dma_start(y_dram[bass.ds(j.value(P), P)], yo[par][:, :]).then_inc(s_yst[par], 16)

            def both(act, j, par):
                step(act, j, par, False)
                store(act, j.before(1), 1 - par)

            step(act, At(None, 0, 0), 0, True)
            both(act, At(None, 0, 1), 1)
            both(act, At(None, 0, 2), 0)
            with act.Fori(0, (TILES - 5) // 2) as i:
                both(act, At(i, 2, 3), 1)
                both(act, At(i, 2, 4), 0)
            both(act, At(None, 0, TILES - 2), 1)
            both(act, At(None, 0, TILES - 1), 0)
            store(act, At(None, 0, TILES - 1), 0)

        @block.vector
        def _(dve):
            dve.wait_ge(s_init, 1)
            dve.tensor_copy(bv_all[:, :], MA[:, 0:C]).then_inc(s_bias, 1)
            dve.tensor_copy(cols[:, 4 * CT + 2:4 * CT + 4], MA[:, C:C + 2]).then_inc(s_bias, 1)
            dve.wait_ge(s_tanh, 1)
            dve.tensor_scalar(bog_c, bo_c, tg_c[:, 0:1], None, ALU.mult).then_inc(s_bog, 1)
            dve.wait_ge(s_bog, 1)

            def attention(dve, g, guard):
                dve.sem_inc(g.c_free, 1)
                dve.sem_inc(g.on, 1)
                if not guard:
                    dve.memset(ok[:, :], 1.0).then_inc(g.ok, 1)

                def rest(b, m, n=1):
                    return res[:, bass.ds(b.value(CT * T, m * T), n * T)]

                def slot(dve, t, par, a, b_, c):
                    bb, bc = t.before(1), t.before(2)
                    if b_ and guard:
                        wait(dve, g.turned, bb, 1)
                        for u in range(UM):
                            wait(dve, g.raw, bb, UM, u + 1)
                            dve.tensor_reduce(maxima[:, 2 * u:2 * u + 2],
                                              S[u % 2][:, :].rearrange("p (n t) -> p n t", n=2), AX_X, ALU.max)\
                                .then_inc(g.top, 1)
                        wait(dve, g.turned, bb, 1, 1)
                        wait(dve, g.shst, bb, 16)
                        dve.tensor_scalar(shift_t[:, :], O[0][0:H * TT, 0:P], -1.0 / SHIFT, None, ALU.mult)\
                            .then_inc(g.shift, 1)
                    if c:
                        for m in range(CT):
                            dve.tensor_scalar(rest(bc, m), rest(bc, m), bog_c[:, m:m + 1], None, ALU.add)\
                                .then_inc(g.xb, 1)
                    if c:
                        wait(dve, g.zl, bc, 16 * GH, 16 * GH)
                        if not guard:
                            for n, (bound, op) in enumerate(((Z_LEAST, ALU.is_ge), (Z_MOST, ALU.is_le))):
                                wait(dve, g.ok, bc, 2, 1 + n)
                                dve.scalar_tensor_tensor(out=ok[:, :], in0=zl[:, :], scalar=bound,
                                                         in1=ok[:, :], op0=op, op1=ALU.mult).then_inc(g.ok, 1)
                        dve.reciprocal(zr[:, :], zl[:, :]).then_inc(g.rz, 1)
                    if a:
                        wait(dve, g.xc, t, 32, 32, s_tanh)
                        for m in range(CT):
                            dve.bn_stats(stats[:, m, :], rest(t, m)).then_inc(g.bst, 1)
                        for m in range(CT):
                            wait(dve, g.bst, t, CT, m + 1, s_tanh)
                            dve.bn_aggr(mv[:, m, :], stats[:, m, :]).then_inc(g.mv, 1)
                    for v in range(VS):
                        what = EXTRA.get(v)
                        if a and v == 1:
                            wait(dve, g.rstd, t, 1, 1)
                            wait(dve, g.a_full, t, NA)
                            for m in range(CT):
                                dve.tensor_scalar(xn[:, m, :], rest(t, m), mv[:, m, 0:1], rstd[:, m:m + 1],
                                                  ALU.subtract, ALU.mult).then_inc(g.xn, 1)
                        if c and v == ON_AT:
                            wait(dve, g.oz, bc, 16 * 16, 16 * 16 + 16)
                            dve.tensor_tensor(on[:, :, :], oc[:, :, :], zc[:, :, :], ALU.mult).then_inc(g.on, 1)
                        if a and what in A_USES:
                            wait(dve, g.a_full, t, NA, A_USES[what] + 1)
                            m = int(what[1])
                            if what[0] in "qk":
                                f, bias, lo = (qf, bq_c, g.ql) if what[0] == "q" else (kf, bk_c, g.kl)
                                wait(dve, lo, t, 1)
                                dve.tensor_scalar(f[:, m, :], MA[:, :], bias[:, m:m + 1], None, ALU.add)\
                                    .then_inc(g.a_free, 1)
                            else:
                                if m == 0:
                                    wait(dve, g.pv, t, VS, -VS)
                                for i in range(2):
                                    last = dve.tensor_tensor(
                                        V[par][:, 2 * m + i, :, 0:DK],
                                        MA[:, i * C:(i + 1) * C].rearrange("p (h c) -> p h c", h=H),
                                        bv_all[:, :].rearrange("p (h c) -> p h c", h=H), ALU.add)
                                last.then_inc(g.a_free, 1)
                        if c and what in C_USES:
                            wait(dve, g.c_full, bc, NCU, C_USES[what] + 1)
                            if what[0] == "o":
                                m = int(what[1])
                                wait(dve, g.xb, bc, CT, m + 1)
                                dve.scalar_tensor_tensor(out=rest(bc, m), in0=MC[:, :], scalar=tg_c[:, 0:1],
                                                         in1=rest(bc, m), op0=ALU.mult, op1=ALU.add).then_inc(g.c_free, 1)
                            elif what[0] == "t":
                                dve.tensor_copy(xT2[:, int(what[1]), :], MC[:, :]).then_inc(g.c_free, 1)
                            else:
                                dve.tensor_copy(logits[:, bass.ds(bc.value(CT * NE), CT * NE)], MC[:, 0:CT * NE])\
                                    .then_inc(g.c_free, 1)
                            if what == "o1":
                                for m in range(CT):
                                    wait(dve, g.c_free, bc, NCU, m + 2, s_tanh)
                                    dve.bn_stats(stats2[:, m, :], rest(bc, m)).then_inc(g.bst2, 1)
                                for m in range(CT):
                                    wait(dve, g.bst2, bc, CT, m + 1, s_tanh)
                                    dve.bn_aggr(mv2[:, m, :], stats2[:, m, :]).then_inc(g.mv2, 1)
                        if c and v == XN2_AT:
                            wait(dve, g.rstd2, bc, 1, 1)
                            wait(dve, g.xnst, bc, 16, 16)
                            for m in range(CT):
                                dve.tensor_scalar(xn2[:, m, :], rest(bc, m), mv2[:, m, 0:1], rstd2[:, m:m + 1],
                                                  ALU.subtract, ALU.mult).then_inc(g.xn2, 1)
                        if b_ and v % TT == TT - 1:
                            g4 = v // TT
                            wait(dve, g.pv, bb, VS, v + 1)
                            wait(dve, g.oz, bb, 16 * 16, 16 - 16 * 16)
                            dve.tensor_copy(osum[1 - par][:, g4, :], O[g4 % 2][:, :]).then_inc(g.os, 1)

                slots(dve, slot)
                if not guard:
                    dve.wait_ge(g.ok, 2 * B + 1)
                    dve.tensor_reduce(ok_min[:, :], ok[:, :], AX_X, ALU.min)\
                        .then_inc(s_okall, 1)
                    dve.wait_ge(s_oksum, 1)
                    dve.tensor_scalar(bad[:, :], MC[:, 0:1], P - 0.5, None, ALU.is_lt).then_inc(s_bad, 1)
                dve.wait_ge(g.xnst, 16 * B + 16)

            both_runs(dve, attention)

            steps = [0]

            def done(ins):
                steps[0] += 1
                ins.then_inc(s_r, 1)
                return steps[0]

            def then(n):
                dve.wait_ge(s_r, n)

            dve.sem_inc(s_done, 1)
            dve.wait_ge(s_done, 2)
            for n in range(NT):
                last = done(dve.max(top8[:, n, :], logits[:, n * NE:(n + 1) * NE]))
            then(last)
            for n in range(NT):
                last = done(dve.max_index(idx8[:, n, :], top8[:, n, :], logits[:, n * NE:(n + 1) * NE]))
            dve.tensor_tensor(dl[:, :], top8[:, :, 1], top8[:, :, 0], ALU.subtract).then_inc(s_wexp, 1)
            then(last)
            last = done(dve.tensor_copy(idxf[:, :, :], idx8[:, :, 0:TOP].rearrange("p n k -> p k n")))
            then(last)
            dve.wait_ge(s_pool_c, 11)
            e_row = iota_f[:, 0:NE].unsqueeze(1).to_broadcast([P, NT, NE])
            for k in range(TOP):
                last = done(dve.tensor_tensor(onehot[:, k], e_row, idxf[:, k].unsqueeze(2).to_broadcast([P, NT, NE]),
                                              ALU.is_equal))
            then(last)
            ranks[0] = done(dve.tensor_tensor(picks[:, :, :], onehot[:, 0], onehot[:, 1], ALU.add))
            dve.wait_ge(s_wexp, 2)
            last = done(dve.tensor_scalar(el1[:, :], el[:, :], 1.0, None, ALU.add))
            then(last)
            last = done(dve.reciprocal(cw[:, 0], el1[:, :]))
            then(last)
            last = done(dve.tensor_tensor(cw[:, 1], cw[:, 0], el[:, :], ALU.mult))
            then(last)
            last = done(dve.tensor_scalar(cwg[:, :, :], cw[:, :, :], tg_c[:, 1:2], None, ALU.mult))
            dve.wait_ge(s_rank, 1)
            last = done(dve.tensor_copy(count_et[:, :].rearrange("p (e n) -> p e n", e=NE),
                                        MC[:, 0:NT * NE].rearrange("p (n e) -> p e n", e=NE)))
            then(last)
            last = done(dve.tensor_tensor_scan(upto_et[:, :], keep_et[:, :], count_et[:, :], 0.0, ALU.mult, ALU.add))
            then(last)
            last = done(dve.tensor_tensor(prev_et[:, :], upto_et[:, :], count_et[:, :], ALU.subtract))
            last = done(dve.tensor_scalar(tot_f[:, :], upto_et[:, NT - 1::NT], float(P - 1), None, ALU.add))
            then(last)
            last = done(dve.tensor_copy(tot_i[:, :], tot_f[:, :]))
            then(last)
            last = done(dve.tensor_scalar(ntl_i[:, :], tot_i[:, :], 7, None, ALU.logical_shift_right))
            then(last)
            last = done(dve.tensor_copy(ntl[:, :], ntl_i[:, :]))
            then(last)
            last = done(dve.tensor_tensor_scan(endt[:, :], ones[:, 0:NE], ntl[:, :], 0.0, ALU.mult, ALU.add))
            then(last)
            last = done(dve.tensor_tensor(startt[:, :], endt[:, :], ntl[:, :], ALU.subtract))
            then(last)
            last = done(dve.scalar_tensor_tensor(
                out=prev_et[:, :].rearrange("p (e n) -> p e n", e=NE),
                in0=startt[:, :].unsqueeze(2).to_broadcast([P, NE, NT]), scalar=float(P),
                in1=prev_et[:, :].rearrange("p (e n) -> p e n", e=NE), op0=ALU.mult, op1=ALU.add))
            then(last)
            last = done(dve.tensor_tensor(slot_e[:, :, :], MA[:, 0:NT * NE].rearrange("p (n e) -> p n e", e=NE),
                                          prev_et[:, :].rearrange("p (e n) -> p n e", e=NE), ALU.add))
            then(last)
            for k in range(TOP):
                last = done(dve.tensor_tensor(slot_m[:, k], onehot[:, k], slot_e[:, :, :], ALU.mult))
            then(last)
            last = done(dve.tensor_reduce(slot_f[:, :], slot_m[:, :, :, :].rearrange("p k n e -> p (k n) e"), AX_X,
                                          ALU.add))
            then(last)
            last = done(dve.tensor_copy(slot_i[:, :], slot_f[:, :]))
            then(last)
            last = done(dve.tensor_scalar(til_i[:, :], slot_i[:, :], 7, None, ALU.logical_shift_right))
            last = done(dve.tensor_scalar(row_i[:, :], slot_i[:, :], P - 1, None, ALU.bitwise_and))
            then(last)
            last = done(dve.tensor_copy(til_f[:, :], til_i[:, :]))
            last = done(dve.tensor_copy(row_f[:, :], row_i[:, :]))
            then(last)
            PAIRS = TOP * NT
            last = done(dve.tensor_tensor(til_hot[:, :, :], iota_f[:, 0:TILES].unsqueeze(1).to_broadcast([P, PAIRS, TILES]),
                                          til_f[:, :].unsqueeze(2).to_broadcast([P, PAIRS, TILES]), ALU.is_equal))
            then(last)
            last = done(dve.tensor_tensor(til_tok[:, :, :], til_hot[:, :, :],
                                          tok_f[:, :].unsqueeze(2).to_broadcast([P, PAIRS, TILES]), ALU.mult))
            last = done(dve.tensor_tensor(row_hot[:, :, :], iota_f[:, :].unsqueeze(1).to_broadcast([P, PAIRS, P]),
                                          row_f[:, :].unsqueeze(2).to_broadcast([P, PAIRS, P]), ALU.is_equal))
            hots[0] = last
            last = done(dve.tensor_tensor(le[:, :, :], endt[:, :].unsqueeze(1).to_broadcast([P, TILES, NE]),
                                          iota_f[:, 0:TILES].unsqueeze(2).to_broadcast([P, TILES, NE]), ALU.is_le))
            then(last)
            last = done(dve.tensor_reduce(et_f[:, :], le[:, :, :], AX_X, ALU.add))
            then(last)
            last = done(dve.tensor_scalar(et_f[:, :], et_f[:, :], float(NE - 1), None, ALU.min))
            then(last)
            last = done(dve.tensor_copy(et_i[:, :], et_f[:, :]))
            last = done(dve.tensor_scalar(table[:, 0:TILES], et_f[:, :], 1.0, 48.0, ALU.add, ALU.mult))
            last = done(dve.tensor_scalar(table[:, 2 * TILES:2 * TILES + NE], endt[:, :], 1.0, None, ALU.add))
            then(last)
            last = done(dve.tensor_scalar(eb_i[:, :], et_i[:, :], EB - 1, None, ALU.bitwise_and))
            then(last)
            last = done(dve.tensor_copy(et_f[:, :], eb_i[:, :]))
            then(last)
            dve.tensor_scalar(table[:, TILES:2 * TILES], et_f[:, :], float(WCOL), None, ALU.mult).then_inc(s_table, 1)
            dve.wait_ge(s_tab, 1)
            dve.tensor_copy(slot_tok[:, :], MC[:, 0:TILES]).then_inc(s_tok, 1)

            def x_out(dve, j, par):
                wait(dve, s_xt, j, 1, 1)
                if not (j.i is None and j.add < 2):
                    wait(dve, s_h, j, 1, -1)
                dve.tensor_copy(xT[par][:, :, :], xt_ps.rearrange("p (k n) -> p k n", n=P)).then_inc(s_xT, 1)

            def step(dve, j, par, nxt):
                if nxt:
                    x_out(dve, At(j.i, j.mul, j.add + 1), 1 - par)
                wait(dve, s_silu, j, 1, 1)
                if not (j.i is None and j.add < 1):
                    wait(dve, s_ht, j, 1, -1)
                dve.tensor_tensor(hh[par][:, :], h3_ps, act1[par][:, :], ALU.mult).then_inc(s_hh, 1)
                wait(dve, s_ht, j, 1, 1)
                if not (j.i is None and j.add < 2):
                    wait(dve, s_y, j, 1)
                dve.tensor_copy(hT[par][:, 0:FT - 1, :],
                                ht_ps[:, 0:(FT - 1) * P].rearrange("p (k n) -> p k n", n=P)).then_inc(s_hT, 1)
                dve.tensor_copy(hT[par][0:FL, FT - 1, :], ht_ps[0:FL, (FT - 1) * P:FT * P]).then_inc(s_hT, 1)

            x_out(dve, At(None, 0, 0), 0)
            for j in range(3):
                step(dve, At(None, 0, j), j % 2, True)
            with dve.Fori(0, (TILES - 5) // 2) as i:
                step(dve, At(i, 2, 3), 1, True)
                step(dve, At(i, 2, 4), 0, True)
            step(dve, At(None, 0, TILES - 2), 1, True)
            step(dve, At(None, 0, TILES - 1), 0, False)

            for n in range(NT):
                m = n % CB
                dve.wait_ge(s_gy[m], 32 * (n // CB + 1))
                if n >= CB:
                    dve.wait_ge(s_out[m], 16 * (n // CB))
                dve.scalar_tensor_tensor(out=o1[m][:, :], in0=y0[m][:, :], scalar=cwg[:, 0, n:n + 1],
                                         in1=res[:, n * T:(n + 1) * T], op0=ALU.mult, op1=ALU.add).then_inc(s_o1, 1)
                dve.wait_ge(s_o1, n + 1)
                dve.scalar_tensor_tensor(out=o2[m][:, :], in0=y1[m][:, :], scalar=cwg[:, 1, n:n + 1],
                                         in1=o1[m][:, :], op0=ALU.mult, op1=ALU.add).then_inc(s_o2, 1)

        @block.tensor
        def _(pe):
            pe.wait_ge(s_const, 16 * NCONST)
            pe.wait_ge(s_pool_c, 5)
            pe.matmul(MA[:, 0:C], ones[0:1, :], bv_r, start=True, stop=True)
            pe.matmul(MA[:, C:C + 2], ones[0:1, :], g_r, start=True, stop=True).then_inc(s_init, 1)
            pe.wait_ge(s_bias, 2)

            def attention(pe, g, guard):
                def scores(b, par, v):
                    g4, st = divmod(v, TT)
                    if v == 0:
                        wait(pe, g.qk, b, 16 * 4 * PARTS, 16 * 4 * PARTS)
                    for n in range(2):
                        u = 2 * v + n
                        wait(pe, g.exp, b, 2 * VS, u - 1)
                        for s in range(2):
                            r0 = 64 * s
                            last = pe.matmul(S[u % 2][:, s * T:(s + 1) * T],
                                             K[par][r0:r0 + PARTS * DK + 1, 2 * g4 + n, st * P:(st + 1) * P],
                                             Q[par][r0:r0 + PARTS * DK + 1, 2 * g4 + n, :], start=True, stop=True)
                        last.then_inc(g.full, 1)

                def row_maxima(b, par):
                    wait(pe, g.qk, b, 16 * 4 * PARTS, 16 * 4 * PARTS)
                    wait(pe, g.exp, b, 2 * VS)
                    for u in range(UM):
                        h = u // (TT // 2)
                        r0 = 64 * (h % 2)
                        wait(pe, g.top, b, UM, u - 1)
                        for n in range(2):
                            tt = 2 * (u % (TT // 2)) + n
                            last = pe.matmul(S[u % 2][:, n * T:(n + 1) * T],
                                             Q[par][r0:r0 + PARTS * DK, h // 2, tt * P:(tt + 1) * P],
                                             K[par][r0:r0 + PARTS * DK, h // 2, :], start=True, stop=True)
                        last.then_inc(g.raw, 1)
                    wait(pe, g.top, b, UM, UM)
                    wait(pe, g.os, b, GROUPS, 0, s_bias)
                    pe.transpose(O[0][0:H * TT, 0:P], maxima[:, :], ident[:, :]).then_inc(g.turned, 1)
                    wait(pe, g.shld, b, 32, 32)

                def values(b, par, v):
                    g4, st = divmod(v, TT)
                    if v == 0:
                        wait(pe, g.a_free, b, NA, A_USES["v1"] + 1)
                        pe.wait_ge(s_vone, 2)
                    wait(pe, g.exp, b, 2 * VS, 2 * v + 2)
                    if st == 0:
                        wait(pe, g.os, b, GROUPS, g4 - 1)
                    for j in range(GH):
                        u = 2 * v + j // 2
                        last = pe.matmul(O[g4 % 2][2 * DK * j:2 * DK * (j + 1), :], V[par][:, st, GH * g4 + j, :],
                                         prob[:, u % RING, (j % 2) * T:(j % 2 + 1) * T],
                                         start=(st == 0), stop=(st == TT - 1), tile_position=(0, 2 * DK * j))
                    last.then_inc(g.pv, 1)

                def project(t, par, what):
                    m = int(what[1])
                    wait(pe, g.a_free, t, NA, A_USES[what])
                    if what[0] == "v":
                        for i in range(2):
                            st = 2 * m + i
                            for k in range(CT):
                                last = pe.matmul(MA[:, i * C:(i + 1) * C], ctx_sb[par][:, k, st * P:(st + 1) * P],
                                                 wv[:, k, :], start=(k == 0), stop=(k == CT - 1))
                    else:
                        if what == "k0":
                            wait(pe, g.xc, t, 32, 32)
                        if what == "q0":
                            wait(pe, g.xn, t, CT, CT)
                        w, src = (wq, xn) if what[0] == "q" else (wk, ctx_sb[par])
                        for k in range(CT):
                            last = pe.matmul(MA[:, :], w[:, k, m * P:(m + 1) * P], src[:, k, :],
                                             start=(k == 0), stop=(k == CT - 1))
                    last.then_inc(g.a_full, 1)

                def output(b, what):
                    wait(pe, g.c_free, b, NCU, C_USES[what] + 1)
                    if what[0] == "o":
                        m = int(what[1])
                        if m == 0:
                            wait(pe, g.on, b, 1, 2)
                        for k in range(CT):
                            last = pe.matmul(MC[:, :], wo[:, k, m * P:(m + 1) * P], on[:, k, :],
                                             start=(k == 0), stop=(k == CT - 1))
                    elif what[0] == "t":
                        m = int(what[1])
                        wait(pe, g.xn2, b, CT, m + 1)
                        for k in range(TT):
                            last = pe.transpose(MC[:, k * P:(k + 1) * P], xn2[:, m, k * P:(k + 1) * P], ident[:, :])
                    else:
                        for m in range(CT):
                            for k in range(TT):
                                last = pe.matmul(MC[:, m * NE:(m + 1) * NE], xT2[:, m, k * P:(k + 1) * P], gate[:, k, :],
                                                 start=(k == 0), stop=(k == TT - 1))
                    last.then_inc(g.c_full, 1)

                def slot(pe, t, par, a, b_, c):
                    bb, bc = t.before(1), t.before(2)
                    first = t.i is None and t.add == 1
                    last_b = t.i is None and t.add == B
                    if b_ and guard:
                        row_maxima(bb, 1 - par)
                    if b_ and (first or guard):
                        scores(bb, 1 - par, 0)
                    for v in range(VS):
                        if b_ and v + 1 < VS:
                            scores(bb, 1 - par, v + 1)
                        what = EXTRA.get(v)
                        if a and what in A_USES:
                            project(t, par, what)
                        if c and what in C_USES:
                            output(bc, what)
                        if b_:
                            if v == VS - 1 and not last_b and not guard:
                                scores(t, par, 0)
                            values(bb, 1 - par, v)

                slots(pe, slot)
                pe.wait_ge(g.c_free, NCU * B + 1)
                if not guard:
                    pe.wait_ge(s_okall, 1)
                    pe.matmul(MC[:, 0:1], ones[:, :], ok_min[:, :], start=True, stop=True).then_inc(s_oksum, 1)
                pe.wait_ge(g.os, GROUPS * B)

            both_runs(pe, attention)

            pe.sem_inc(s_done, 1)
            pe.wait_ge(s_r, ranks[0])
            pe.matmul(MA[:, 0:NT * NE], below[:, :], picks[:, :, :].rearrange("p n e -> p (n e)"), start=True, stop=True)
            pe.matmul(MC[:, 0:NT * NE], ones[:, :], picks[:, :, :].rearrange("p n e -> p (n e)"), start=True, stop=True)\
                .then_inc(s_rank, 1)
            pe.wait_ge(s_r, hots[0])
            for n in range(TOP * NT):
                last = pe.matmul(MC[:, 0:TILES], row_hot[:, n, :], til_tok[:, n, :], start=(n == 0),
                                 stop=(n == TOP * NT - 1))
            last.then_inc(s_tab, 1)
            pe.wait_ge(s_table, 1)
            pe.sem_inc(s_y, 1)

            def turn_x(j, par):
                pe.wait_ge(s_xg[par], At(j.i, j.mul // 2, j.add // 2).value(16, 16))
                wait(pe, s_xT, j, 1)
                for k in range(TT):
                    last = pe.transpose(xt_ps[:, k * P:(k + 1) * P], xg[par][:, k * P:(k + 1) * P], ident[:, :])
                last.then_inc(s_xt, 1)

            def hidden(j, par):
                need = pe.value_load(table[0:1, bass.ds(j.value(), 1)], min_val=48, max_val=48 * NE)
                off = pe.value_load(table[0:1, bass.ds(j.value(1, TILES), 1)], min_val=0, max_val=(EB - 1) * WCOL)
                pe.wait_ge(s_wr, need)
                wait(pe, s_xT, j, 1, 1)
                wait(pe, s_hh, j, 1)
                for k in range(TT):
                    for n, ps in enumerate((h1_ps, h3_ps)):
                        last = pe.matmul(ps, xT[par][:, k, :], W[:, bass.ds(off + (2 * k + n) * F, F)],
                                         start=(k == 0), stop=(k == TT - 1))
                last.then_inc(s_h, 1)

            def turn_h(j, par):
                wait(pe, s_hh, j, 1, 1)
                wait(pe, s_hT, j, 2)
                for k in range(FT):
                    n = P if k < FT - 1 else FL
                    last = pe.transpose(ht_ps[0:n, k * P:(k + 1) * P], hh[par][:, k * P:k * P + n], ident[:, :])
                last.then_inc(s_ht, 1)

            def down(j, par):
                off = pe.value_load(table[0:1, bass.ds(j.value(1, TILES), 1)], min_val=0, max_val=(EB - 1) * WCOL)
                wait(pe, s_hT, j, 2, 2)
                wait(pe, s_yo, j, 1)
                for k in range(FT):
                    n = P if k < FT - 1 else FL
                    last = pe.matmul(y_ps[:, :], hT[par][0:n, k, :], W[0:n, bass.ds(off + TT * 2 * F + k * T, T)],
                                     start=(k == 0), stop=(k == FT - 1))
                last.then_inc(s_y, 1)

            def step(j, par, first, more):
                hidden(j, par)
                if more:
                    turn_x(At(j.i, j.mul, j.add + 1), 1 - par)
                if not first:
                    down(j.before(1), 1 - par)
                turn_h(j, par)

            turn_x(At(None, 0, 0), 0)
            for j in range(3):
                step(At(None, 0, j), j % 2, j == 0, True)
            with pe.Fori(0, (TILES - 5) // 2) as i:
                step(At(i, 2, 3), 1, False, True)
                step(At(i, 2, 4), 0, False, True)
            step(At(None, 0, TILES - 2), 1, False, True)
            step(At(None, 0, TILES - 1), 0, False, False)
            down(At(None, 0, TILES - 1), 0)


def kernel(**inputs):
    import numpy as np
    import concourse.bacc as bacc
    from concourse.bass_utils import run_bass_kernel_spmd

    a = {k: np.asarray(v) for k, v in inputs.items()}
    w1, w3, w2 = a["L0_ffn_w1"], a["L0_ffn_w3"], a["L0_ffn_w2"]
    arrays = {
        "x": a["x"], "ctx_in": a["ctx_2048"], "g_xattn": a["g_xattn"], "g_ffn": a["g_ffn"],
        "WqT": a["L0_xattn_Wq"].T, "bq": a["L0_xattn_bq"], "WkT": a["L0_xattn_Wk"].T, "bk": a["L0_xattn_bk"],
        "WvT": a["L0_xattn_Wv"].T, "bv": a["L0_xattn_bv"], "WoT": a["L0_xattn_Wo"].T, "bo": a["L0_xattn_bo"],
        "gateT": a["L0_ffn_gate_w"].T,
        "w13T": np.concatenate([w1.transpose(0, 2, 1), w3.transpose(0, 2, 1)], axis=2),
        "w2T": w2.transpose(0, 2, 1),
    }
    for k in ("bq", "bk", "bo"):
        arrays[k] = arrays[k].reshape(-1, P).T
    arrays = {k: np.ascontiguousarray(v) for k, v in arrays.items()}
    nc = bacc.Bacc("TRN2", target_bir_lowering=False, num_devices=1)
    args = [nc.dram_tensor(k, v.shape, mybir.dt.from_np(v.dtype), kind="ExternalInput").ap()
            for k, v in arrays.items()]
    out = nc.dram_tensor("out", a["x"].shape, F32, kind="ExternalOutput").ap()
    flamingo_kernel(nc, *args, out)
    r = run_bass_kernel_spmd(nc, [arrays], core_ids=[0])
    return r.results[0]["out"]
```

```python
from contextlib import ExitStack

import concourse.bass as bass
from concourse import mybir

ALU = mybir.AluOpType
ACT = mybir.ActivationFunctionType
AX_X = mybir.AxisListType.X
F32 = mybir.dt.float32
F16 = mybir.dt.float16
I32 = mybir.dt.int32
U32 = mybir.dt.uint32
U16 = mybir.dt.uint16

P = 128
EPS = 1e-5


class At:

    def __init__(self, i, mul, add):
        self.i, self.mul, self.add = i, mul, add

    def value(self, k=1, c=0):
        if self.i is None:
            return k * self.add + c
        return self.i * (k * self.mul) + (k * self.add + c)

    def before(self, n):
        return At(self.i, self.mul, self.add - n)


def wait(eng, sem, at, k, c=0, alone=None):
    if at.i is None and k * at.add + c <= 0:
        return
    assert k * at.add + c > 0, "a wait against nothing in a loop's first round"
    value = at.value(k, c)
    if alone is not None and at.i is not None:
        value = eng.to_reg(value)
        eng.wait_ge(alone, 1)
    eng.wait_ge(sem, value)


class Signals:

    def __init__(self, sem):
        self.xc = sem("xc")
        self.bst, self.mv, self.veps, self.rstd, self.xn = sem("bst"), sem("mv"), sem("veps"), sem("rstd"), sem("xn")
        self.bst2, self.mv2, self.veps2, self.rstd2, self.xn2 = (
            sem("bst2"), sem("mv2"), sem("veps2"), sem("rstd2"), sem("xn2"))
        self.a_full, self.a_free = sem("a_full"), sem("a_free")
        self.c_full = sem("c_full")
        self.c_free = sem("c_free")
        self.qh, self.ql, self.kh, self.kl = sem("qh"), sem("ql"), sem("kh"), sem("kl")
        self.qkst = sem("qkst")
        self.qk = sem("qk")
        self.full = sem("full")
        self.exp = sem("exp")
        self.pv = sem("pv")
        self.os = sem("os")
        self.zl = sem("zl")
        self.rz = sem("rz")
        self.zst = sem("zst")
        self.oz = sem("oz")
        self.on = sem("on")
        self.xb = sem("xb")
        self.outst = sem("outst")
        self.x2h, self.x2l = sem("x2h"), sem("x2l")
        self.xnst = sem("xnst")
        self.ok = sem("ok")
        self.raw = sem("raw")
        self.top = sem("top")
        self.turned = sem("turned")
        self.shift = sem("shift")
        self.shst = sem("shst")
        self.shld = sem("shld")


def flamingo_kernel(nc, x, ctx_in, g_xattn, g_ffn, WqT, bq, WkT, bk, WvT, bv, WoT, bo, gateT, wall, out):
    B, C, T = x.shape
    H, DK = 16, C // 16
    CT, TT = C // P, T // P
    NE = gateT.shape[1]
    WCOL = wall.shape[2]
    FT = 3
    F = (WCOL - FT * T) // (2 * TT)
    assert -(-F // P) == FT
    FL = F - (FT - 1) * P
    TOP = 2
    TOK = B * C
    NT = TOK // P
    TILES = (TOP * TOK + NE * (P - 1)) // P
    SCALE = DK ** -0.5
    ZW = H * T // P
    G = H // 2
    SHIFT = 64.0
    PARTS = 3
    GROUPS, GH = H // 4, 4
    RING = 4
    UM = H * TT // 2
    Z_LEAST, Z_MOST = 1e-20, 1e30
    LO = 2048.0
    TR = 4
    EB = 4
    W2 = TT * 2 * F
    WS, HS = 256.0, 16.0
    WQ = WCOL // 4

    q_dram = nc.dram_tensor("q_parts", [2, C, T], F16).ap()
    k_dram = nc.dram_tensor("k_parts", [2, C, T], F16).ap()
    z_dram = nc.dram_tensor("inverse_sums", [GH, GROUPS, T], F32).ap()
    shift_dram = nc.dram_tensor("shift_rows", [H, T], F16).ap()
    xn_dram = nc.dram_tensor("tokens_normed", [TOK, 2 * T], F16).ap()
    w_dram = nc.dram_tensor("weight_parts", [NE, P, 2, WCOL], F16).ap()

    x_v = x.rearrange("b (m p) t -> b p m t", p=P)
    c_v = ctx_in.rearrange("b (m p) t -> b p m t", p=P)
    out_v = out[0:TOK].rearrange("(b m p) t -> b p m t", b=B, p=P)

    top = ExitStack()
    with top:
        def sb(name, shape, dt=F32, stack=top):
            return stack.enter_context(nc.sbuf_tensor(name, shape, dt))

        def sem(name):
            return top.enter_context(nc.semaphore(name))

        res = sb("residual", [P, NT * T])
        ident = sb("ident", [P, P])
        ident16 = sb("ident16", [P, P], F16)
        ones = sb("ones", [P, P])
        below = sb("below", [P, P])
        gate = sb("gate", [P, TT, NE])
        lgT = sb("lgT", [NE, C])
        logits = sb("logits", [P, NT * NE])
        rows = sb("rows", [1, 2 * C + 2])
        cols = sb("cols", [P, 4 * CT + 4])
        ok = sb("ok", [P, ZW])
        ok_min = sb("ok_min", [P, 1])
        bad = sb("bad", [P, 1], U16)
        maxima = sb("maxima", [P, H * TT])
        shift_t = sb("shift_t", [H * TT, P], F16)
        neg_half = sb("neg_half", [P, CT])

        att = ExitStack()
        ctx_sb = [sb(f"ctx{i}", [P, CT, T], F32, att) for i in range(2)]
        xn = sb("xn", [P, CT, T], F32, att)
        qf = sb("qf", [P, CT, T], F32, att)
        kf = sb("kf", [P, CT, T], F32, att)
        qs = sb("qs", [P, 2, CT, T], F16, att)
        ks = sb("ks", [P, 2, CT, T], F16, att)
        Q = [sb(f"Q{i}", [P, G, T], F16, att) for i in range(2)]
        K = [sb(f"K{i}", [P, G, T], F16, att) for i in range(2)]
        V = [sb(f"V{i}", [P, TT, H, 2 * DK], F32, att) for i in range(2)]
        prob = sb("prob", [P, RING, 2 * T], F32, att)
        osum = [sb(f"osum{i}", [P, GROUPS, T], F32, att) for i in range(2)]
        oc = sb("oc", [P, CT, T], F32, att)
        zc = sb("zc", [P, CT, T], F32, att)
        zl = sb("zl", [P, ZW], F32, att)
        zr = sb("zr", [P, ZW], F32, att)
        on = sb("on", [P, CT, T], F32, att)
        xn2 = sb("xn2", [P, CT, T], F32, att)
        xs2 = sb("xs2", [P, 2, CT, T], F16, att)
        wf = [sb(f"wf{i}", [P, WQ], F32, att) for i in range(2)]
        wp = [sb(f"wp{i}", [P, 2, WQ], F16, att) for i in range(2)]
        xT2 = sb("xT2", [P, CT, T], F32, att)
        wq = sb("wq", [P, CT, C], F32, att)
        wk = sb("wk", [P, CT, C], F32, att)
        wv = sb("wv", [P, CT, C], F32, att)
        wo = sb("wo", [P, CT, C], F32, att)
        bv_all = sb("bv_all", [P, C], F32, att)
        stats = sb("stats", [P, CT, 6], F32, att)
        mv = sb("mv", [P, CT, 2], F32, att)
        veps = sb("veps", [P, CT], F32, att)
        rstd = sb("rstd", [P, CT], F32, att)
        stats2 = sb("stats2", [P, CT, 6], F32, att)
        mv2 = sb("mv2", [P, CT, 2], F32, att)
        veps2 = sb("veps2", [P, CT], F32, att)
        rstd2 = sb("rstd2", [P, CT], F32, att)
        att.close()

        top8 = sb("top8", [P, NT, 8])
        idx8 = sb("idx8", [P, NT, 8], U32)
        idxf = sb("idxf", [P, TOP, NT])
        dl = sb("dl", [P, NT])
        el = sb("el", [P, NT])
        el1 = sb("el1", [P, NT])
        cw = sb("cw", [P, TOP, NT])
        cwg = sb("cwg", [P, TOP, NT])
        iota_i = sb("iota_i", [P, P], I32)
        iota_f = sb("iota_f", [P, P])
        tok_i = sb("tok_i", [P, TOP * NT], I32)
        tok_f = sb("tok_f", [P, TOP * NT])
        onehot = sb("onehot", [P, TOP, NT, NE])
        picks = sb("picks", [P, NT, NE])
        count_et = sb("count_et", [P, NE * NT])
        keep_et = sb("keep_et", [P, NE * NT])
        upto_et = sb("upto_et", [P, NE * NT])
        prev_et = sb("prev_et", [P, NE * NT])
        tot_f = sb("tot_f", [P, NE])
        tot_i = sb("tot_i", [P, NE], I32)
        ntl_i = sb("ntl_i", [P, NE], I32)
        ntl = sb("ntl", [P, NE])
        endt = sb("endt", [P, NE])
        startt = sb("startt", [P, NE])
        slot_e = sb("slot_e", [P, NT, NE])
        slot_m = sb("slot_m", [P, TOP, NT, NE])
        slot_f = sb("slot_f", [P, TOP * NT])
        slot_i = sb("slot_i", [P, TOP * NT], I32)
        til_i = sb("til_i", [P, TOP * NT], I32)
        row_i = sb("row_i", [P, TOP * NT], I32)
        til_f = sb("til_f", [P, TOP * NT])
        row_f = sb("row_f", [P, TOP * NT])
        row_hot = sb("row_hot", [P, TOP * NT, P], F16)
        til_tok = sb("til_tok", [P, TOP * NT, 4, TILES], F16)
        w_hi = sb("w_hi", [P, TOP * NT], F16)
        w_rest = sb("w_rest", [P, TOP * NT])
        w_lo = sb("w_lo", [P, TOP * NT], F16)
        slot_tok = sb("slot_tok", [P, TILES], U32)
        slot_out = sb("slot_out", [P, TILES], U32)
        slot_w = sb("slot_w", [P, TILES])
        slot_pad = sb("slot_pad", [P, TILES])
        spare = sb("spare", [P, 2])
        le = sb("le", [P, TILES, NE])
        et_f = sb("et_f", [P, TILES])
        et_i = sb("et_i", [P, TILES], I32)
        eb_i = sb("eb_i", [P, TILES], I32)
        eo_i = sb("eo_i", [P, TILES], I32)
        table = sb("table", [P, 2 * TILES + NE], U16)
        W = sb("W", [P, EB * 2 * WCOL], F16)
        xg = [sb(f"xg{i}", [P, 2 * T], F16) for i in range(TR)]
        xT = [sb(f"xT{i}", [P, 2 * TT, P], F16) for i in range(2)]
        act1 = [sb(f"act1_{i}", [P, F]) for i in range(2)]
        hh = [sb(f"hh{i}", [P, F]) for i in range(2)]
        hs = [sb(f"hs{i}", [P, 2 * F], F16) for i in range(2)]
        hT = [sb(f"hT{i}", [P, 2 * FT, P], F16) for i in range(2)]
        yo = [sb(f"yo{i}", [P, T]) for i in range(TR)]

        S = [top.enter_context(nc.psum_tensor(f"S{i}", [P, 2 * T], F32)) for i in range(2)]
        O = [top.enter_context(nc.psum_tensor(f"O{i}", [P, T], F32)) for i in range(2)]
        MA = top.enter_context(nc.psum_tensor("MA", [P, T], F32))
        MC = top.enter_context(nc.psum_tensor("MC", [P, T], F32))
        h1_ps, h3_ps = S[0][:, 0:F], S[0][:, T:T + F]
        xt_ps, ht_ps = S[1][:, 0:T].bitcast(F16), S[1][:, T:2 * T].bitcast(F16)
        y_ps = O[0]

        bq_c, bk_c, bo_c = (cols[:, n * CT:(n + 1) * CT] for n in range(3))
        bog_c = cols[:, 3 * CT:4 * CT]
        tg_c = cols[:, 4 * CT:4 * CT + 2]
        bv_r = rows[:, 0:C]
        g_r = rows[:, 2 * C:2 * C + 2]

        fast = Signals(lambda name: sem("f_" + name))
        slow = Signals(lambda name: sem("g_" + name))
        s_okall = sem("s_okall")
        s_oksum = sem("s_oksum")
        s_bad = sem("s_bad")
        s_rows = sem("s_rows")
        s_done = sem("s_done")

        def both_runs(eng, attention):
            attention(eng, fast, False)
            eng.wait_ge(s_bad, 1)
            with eng.If(eng.value_load(bad[0:1, 0:1], min_val=0, max_val=1) > 0):
                attention(eng, slow, True)

        NCONST = 4 + 3 + 1 + 2 + 1
        s_const = sem("s_const")
        s_pool_c = sem("s_pool_c")
        s_init = sem("s_init")
        s_bias = sem("s_bias")
        s_tanh = sem("s_tanh")
        s_bog = sem("s_bog")
        s_vone = sem("s_vone")
        A_USES = {n: k for k, n in enumerate(("k0", "k1", "q0", "q1", "v0", "v1"))}
        C_USES = {n: k for k, n in enumerate(("o0", "o1", "t0", "t1", "lg", "lt"))}
        NA, NCU = len(A_USES), len(C_USES)
        EXTRA = {2: "k0", 4: "k1", 5: "q0", 7: "q1", 8: "o0", 9: "v0", 10: "o1", 11: "v1", 12: "t0", 13: "t1",
                 14: "lg", 15: "lt"}
        ON_AT, XN2_AT = 7, 11
        VS = GROUPS * TT

        def quarters(t):
            if t.i is None and t.add == 0:
                steps, experts = (3, 6, 9, 12, 13, 14, 15, 15), (0, 1)
            elif t.i is None and t.add == B:
                steps, experts = (0, 2, 4, 6, 8, 10, 12, 14), (NE - 3, NE - 2)
            elif t.i is None and t.add == B + 1:
                steps, experts = (0, 0, 1, 1), (NE - 1,)
            else:
                steps, experts = (0, 3, 6, 9), (t.before(-1),)
            experts = [e if isinstance(e, At) else At(None, 0, e) for e in experts]
            return [(v, experts[n // 4], n % 4) for n, v in enumerate(steps)]

        def slots(eng, slot):
            slot(eng, At(None, 0, 0), 0, True, False, False)
            slot(eng, At(None, 0, 1), 1, True, True, False)
            with eng.Fori(0, (B - 2) // 2) as i:
                slot(eng, At(i, 2, 2), 0, True, True, True)
                slot(eng, At(i, 2, 3), 1, True, True, True)
            slot(eng, At(None, 0, B), 0, False, True, True)
            slot(eng, At(None, 0, B + 1), 1, False, False, True)

        s_r = sem("s_r")
        s_wexp = sem("s_wexp")
        s_rank = sem("s_rank")
        s_tab = sem("s_tab")
        s_tok = sem("s_tok")
        s_table = sem("s_table")
        s_w = [sem(f"s_w{i}") for i in range(EB)]
        s_wr = sem("s_wr")
        s_wf = [sem(f"s_wf{i}") for i in range(2)]
        s_whi, s_wlo = sem("s_whi"), sem("s_wlo")
        s_wst = [sem(f"s_wst{i}") for i in range(2)]
        s_hi = sem("s_hi")
        s_lo = sem("s_lo")
        s_xg = [sem(f"s_xg{i}") for i in range(TR)]
        s_xt = sem("s_xt")
        s_xT = sem("s_xT")
        s_h = sem("s_h")
        s_silu = sem("s_silu")
        s_hh = sem("s_hh")
        s_ht = sem("s_ht")
        s_hT = sem("s_hT")
        s_y = sem("s_y")
        s_yo = sem("s_yo")
        def tiles(eng, step):
            first = TR - 1
            rounds = (TILES - first - 1) // TR
            for n in range(first):
                step(eng, At(None, 0, n), n)
            with eng.Fori(0, rounds) as i:
                for n in range(first, first + TR):
                    step(eng, At(i, TR, n), n)
            for n in range(first + rounds * TR, TILES):
                step(eng, At(None, 0, n), n)

        s_add = sem("s_add")
        s_stored = sem("s_stored")
        s_spare = sem("s_spare")

        ranks, hots = [0], [0]

        block = top.enter_context(nc.Block())

        @block.sync
        def _(sp):
            for dst, src in ((wk, WkT), (wq, WqT), (wv, WvT), (wo, WoT)):
                sp.dma_start(dst[:, :, :], src.rearrange("(k p) n -> p k n", p=P)).then_inc(s_const, 16)
            for dst, src in ((bq_c, bq), (bk_c, bk), (bo_c, bo)):
                sp.dma_start(dst, src).then_inc(s_const, 16)
            sp.dma_start(bv_r, bv.rearrange("(a n) -> a n", a=1)).then_inc(s_const, 16)
            for n, g in enumerate((g_xattn, g_ffn)):
                sp.dma_start(g_r[:, n:n + 1], g.rearrange("(a n) -> a n", a=1)).then_inc(s_const, 16)
            sp.dma_start(gate[:, :, :], gateT.rearrange("(k p) n -> p k n", p=P)).then_inc(s_const, 16)

            def attention(sp, g, guard):
                sp.sem_inc(g.oz, 16)
                sp.sem_inc(g.xnst, 16)

                def load_batch(b, par):
                    sp.dma_start(res[:, bass.ds(b.value(CT * T), CT * T)].rearrange("p (m t) -> p m t", m=CT),
                                 x_v[bass.ds(b.value(), 1)].rearrange("b p m t -> p (b m) t")).then_inc(g.xc, 16)
                    sp.dma_start(ctx_sb[par][:, :, :],
                                 c_v[bass.ds(b.value(), 1)].rearrange("b p m t -> p (b m) t")).then_inc(g.xc, 16)

                def slot(sp, t, par, a, b_, c):
                    if b_ and guard:
                        bb = t.before(1)
                        wait(sp, g.shld, bb, 32, 0, s_bog)
                        wait(sp, g.shift, bb, 1, 1, s_bog)
                        sp.dma_start(shift_dram.rearrange("h (n p) -> (h n) p", p=P), shift_t[:, :])\
                            .then_inc(g.shst, 16)
                        wait(sp, g.shst, bb, 16, 16, s_bog)
                        for s in range(2):
                            row = 64 * s + PARTS * DK
                            sp.dma_start(Q[1 - par][row:row + 1, :, :],
                                         shift_dram.rearrange("(a g s) t -> s a g t", s=2, a=1)[s]).then_inc(g.shld, 16)
                    if a:
                        wait(sp, g.xc, t, 32, 0, s_bog)
                        wait(sp, g.a_free, t, NA, -NA)
                        load_batch(t, par)
                    if c:
                        bc = t.before(2)
                        wait(sp, g.os, bc, GROUPS, GROUPS, s_bog)
                        wait(sp, g.on, bc, 1, 1)
                        for j in range(GH):
                            sp.dma_start(zl[32 * j:32 * (j + 1), :], osum[par][2 * DK * j + DK:2 * DK * j + DK + 1, :, :])\
                                .then_inc(g.zl, 16)
                        for half in range(2):
                            for j in range(GH):
                                dst0 = 64 * half + DK * j
                                src = osum[par][2 * DK * j:2 * DK * j + DK, half::2, :]
                                sp.dma_start(oc[dst0:dst0 + DK, :, :], src).then_inc(g.oz, 16)
                        wait(sp, g.rz, bc, 1, 1)
                        sp.dma_start(z_dram.rearrange("j g t -> (j g t)").rearrange("(p n) -> p n", p=P), zr[:, :])\
                            .then_inc(g.zst, 16)
                        wait(sp, g.zst, bc, 16, 16)
                        for half in range(2):
                            for j in range(GH):
                                dst0 = 64 * half + DK * j
                                src = z_dram[j:j + 1, half::2, :].to_broadcast([DK, CT, T])
                                sp.dma_start(zc[dst0:dst0 + DK, :, :], src).then_inc(g.oz, 16)
                    if a:
                        wait(sp, g.qk, t, 16 * 4 * PARTS, 0, s_bog)
                        wait(sp, g.kl, t, 1, 1)
                        sp.dma_start(k_dram.rearrange("h (m p) t -> p h m t", p=P), ks[:, :, :, :]).then_inc(g.qkst, 16)
                        wait(sp, g.ql, t, 1, 1)
                        sp.dma_start(q_dram.rearrange("h (m p) t -> p h m t", p=P), qs[:, :, :, :]).then_inc(g.qkst, 16)
                        wait(sp, g.qkst, t, 32, 32, s_bog)
                        wait(sp, g.full, t, 2 * VS, -2 * VS)
                        sp.wait_ge(s_rows, 8)
                        for s in range(2):
                            for r, (qp, kp) in enumerate(((0, 0), (1, 0), (0, 1))):
                                for stack, dram, part in ((Q, q_dram, qp), (K, k_dram, kp)):
                                    src = dram[part].rearrange("(g s c) t -> s c g t", s=2, c=DK)[s]
                                    sp.dma_start(stack[par][64 * s + DK * r:64 * s + DK * (r + 1), :, :], src)\
                                        .then_inc(g.qk, 16)
                    if c:
                        bc = t.before(2)
                        wait(sp, g.c_free, bc, NCU, C_USES["o1"] + 2, s_bog)
                        sp.dma_start(out_v[bass.ds(bc.value(), 1)].rearrange("b p m t -> p (b m) t"),
                                     res[:, bass.ds(bc.value(CT * T), CT * T)].rearrange("p (m t) -> p m t", m=CT))\
                            .then_inc(g.outst, 16)
                        wait(sp, g.x2l, bc, 1, 1, s_bog)
                        dst = xn_dram[bass.ds(bc.value(C), C)].rearrange("(m p) (h t) -> p h m t", p=P, h=2)
                        sp.dma_start(dst, xs2[:, :, :, :]).then_inc(g.xnst, 16)

                slots(sp, slot)
                sp.wait_ge(g.xnst, 16 * B + 16)
                sp.wait_ge(g.outst, 16 * B)

            both_runs(sp, attention)

            sp.sem_inc(s_stored, 1)
            sp.wait_ge(s_pool_c, 5)
            for n in range(TT):
                sp.dma_start(out[TOK:TOK + P, n * P:(n + 1) * P], ones[:, :]).then_inc(s_spare, 16)
            sp.wait_ge(s_done, 2)
            for n in range(2):
                sp.wait_ge(s_wst[n], 16 * 2 * NE)
            for e in range(NE):
                if e == EB:
                    sp.wait_ge(s_table, 1)
                if e >= EB:
                    end = sp.value_load(table[0:1, 2 * TILES + e - EB:2 * TILES + e - EB + 1], min_val=1,
                                        max_val=TILES + 1)
                    sp.wait_ge(s_y, end)
                sp.dma_start(W[:, (e % EB) * 2 * WCOL:(e % EB + 1) * 2 * WCOL],
                             w_dram[e].rearrange("p h n -> p (h n)")).then_inc(s_wr, 16)
                sp.wait_ge(s_wr, 16 * (e + 1))

        @block.gpsimd
        def _(pool):
            pool.memset(ident[:, :], 0.0).then_inc(s_pool_c, 1)
            pool.memset(ones[:, :], 1.0).then_inc(s_pool_c, 1)
            pool.memset(neg_half[:, :], -0.5).then_inc(s_pool_c, 1)
            pool.wait_ge(s_pool_c, 3)
            pool.affine_select(out=ident[:, :], in_=ident[:, :], compare_op=ALU.not_equal, fill=1.0, base=0,
                               pattern=[[-1, P]], channel_multiplier=1).then_inc(s_pool_c, 1)
            pool.affine_select(out=below[:, :], in_=ones[:, :], compare_op=ALU.is_gt, fill=0.0, base=0,
                               pattern=[[1, P]], channel_multiplier=-1).then_inc(s_pool_c, 1)
            pool.wait_ge(s_pool_c, 5)
            pool.tensor_copy(ident16[:, :], ident[:, :]).then_inc(s_vone, 1)
            for i in range(2):
                pool.memset(V[i][:, :, :, DK:2 * DK], 1.0).then_inc(s_vone, 1)

            def attention(pool, g, guard):
                def slot(pool, t, par, a, b_, c):
                    if a:
                        pool.wait_ge(s_pool_c, 5)
                        wait(pool, g.mv, t, CT, CT, s_pool_c)
                        pool.tensor_scalar(veps[:, :], mv[:, :, 1], EPS, None, ALU.add).then_inc(g.veps, 1)
                        wait(pool, g.veps, t, 1, 1)
                        pool.tensor_tensor(rstd[:, :], veps[:, :], neg_half[:, :], ALU.pow).then_inc(g.rstd, 1)
                        for f, parts, hi, lo in ((kf, ks, g.kh, g.kl), (qf, qs, g.qh, g.ql)):
                            wait(pool, hi, t, 1, 1)
                            pool.tensor_tensor(parts[:, 1], f[:, :, :], parts[:, 0], ALU.subtract).then_inc(lo, 1)
                    if c:
                        bc = t.before(2)
                        wait(pool, g.mv2, bc, CT, CT, s_pool_c)
                        pool.tensor_scalar(veps2[:, :], mv2[:, :, 1], EPS, None, ALU.add).then_inc(g.veps2, 1)
                        wait(pool, g.veps2, bc, 1, 1)
                        pool.tensor_tensor(rstd2[:, :], veps2[:, :], neg_half[:, :], ALU.pow).then_inc(g.rstd2, 1)
                        wait(pool, g.x2h, bc, 1, 1)
                        pool.tensor_tensor(xs2[:, 1], xn2[:, :, :], xs2[:, 0], ALU.subtract).then_inc(g.x2l, 1)

                slots(pool, slot)

            both_runs(pool, attention)

            pool.wait_ge(s_done, 2)
            pool.iota(iota_i[:, :], pattern=[[1, P]], base=0, channel_multiplier=0).then_inc(s_pool_c, 1)
            pool.iota(tok_i[:, :], pattern=[[0, TOP], [P, NT]], base=0, channel_multiplier=1).then_inc(s_pool_c, 1)
            pool.memset(keep_et[:, :], 1.0).then_inc(s_pool_c, 1)
            pool.wait_ge(s_pool_c, 8)
            pool.tensor_copy(iota_f[:, :], iota_i[:, :]).then_inc(s_pool_c, 1)
            pool.tensor_copy(tok_f[:, :], tok_i[:, :]).then_inc(s_pool_c, 1)
            pool.memset(keep_et[:, ::NT], 0.0).then_inc(s_pool_c, 1)

            pool.wait_ge(s_tok, 3)
            def gather(j):
                if j >= TR:
                    pool.wait_ge(s_xt, j - TR + 1)
                pool.indirect_dma_start(out=xg[j % TR][:, :], out_offset=None, in_=xn_dram[:, :],
                                        in_offset=bass.IndirectOffsetOnAxis(ap=slot_tok[:, j:j + 1], axis=0))\
                    .then_inc(s_xg[j % TR], 16)

            for j in range(TR):
                gather(j)
            pool.wait_ge(s_spare, 16 * TT)
            pool.wait_ge(s_stored, 1)
            for j in range(TILES):
                pool.wait_ge(s_yo, j + 1)
                if j >= 1:
                    pool.wait_ge(s_add, 16 * j)
                pool.indirect_dma_start(out=out[:, :],
                                        out_offset=bass.IndirectOffsetOnAxis(ap=slot_out[:, j:j + 1], axis=0),
                                        in_=yo[j % TR][:, :], in_offset=None, compute_op=ALU.add)\
                    .then_inc(s_add, 16)
                if j + TR < TILES:
                    gather(j + TR)
            pool.wait_ge(s_add, 16 * TILES)

        @block.scalar
        def _(act):
            act.wait_ge(s_bias, 2)
            act.activation(tg_c, cols[:, 4 * CT + 2:4 * CT + 4], ACT.Tanh).then_inc(s_tanh, 1)

            for i in range(2):
                for r0 in (64 * s + 32 for s in range(2)):
                    one = ones[r0:r0 + 32, 0:1].to_broadcast([32, G * T])
                    for stack, factor in ((Q, 0.0), (K, SHIFT)):
                        act.activation(stack[i][r0:r0 + 32, :, :].rearrange("p g t -> p (g t)"), one, ACT.Copy,
                                       scale=factor).then_inc(s_rows, 1)

            def attention(act, g, guard):
                def load_quarter(e, c):
                    act.dma_start(wf[c % 2][:, :], wall[bass.ds(e.value(), 1), :, c * WQ:(c + 1) * WQ]
                                  .rearrange("e p n -> p (e n)")).then_inc(s_wf[c % 2], 16)

                def store_quarter(e, c):
                    wait(act, s_wlo, e, 4, c + 1, s_bias)
                    act.dma_start(w_dram[bass.ds(e.value(), 1), :, :, c * WQ:(c + 1) * WQ]
                                  .rearrange("e p h n -> p (e h) n"), wp[c % 2][:, :, :]).then_inc(s_wst[c % 2], 16)
                    e, c = (e, c + 2) if c < 2 else (e.before(-1), c - 2)
                    if e.i is not None or e.add < NE:
                        load_quarter(e, c)

                if not guard:
                    for n in range(2):
                        load_quarter(At(None, 0, 0), n)

                def slot(act, t, par, a, b_, c):
                    splits = [] if guard else quarters(t)
                    if not b_:
                        for _, e, c in splits:
                            store_quarter(e, c)
                        return
                    b = t.before(1)
                    for u in range(2 * VS):
                        wait(act, g.full, b, 2 * VS, u + 1)
                        wait(act, g.pv, b, VS, u // 2 - RING // 2 + 1)
                        act.activation(prob[:, u % RING, :], S[u % 2][:, :], ACT.Exp, scale=SCALE).then_inc(g.exp, 1)
                        for v, e, c in splits:
                            if u == 2 * min(v + 2, VS - 1) + 1:
                                store_quarter(e, c)

                slots(act, slot)

            both_runs(act, attention)

            act.wait_ge(s_wexp, 1)
            act.activation(el[:, :], dl[:, :], ACT.Exp).then_inc(s_wexp, 1)

            def gate_tile(act, j, n):
                wait(act, s_h, j, 1, 1)
                if n >= 2:
                    wait(act, s_hh, j, 1, -1)
                act.activation(act1[n % 2][:, :], h1_ps, ACT.Silu, scale=1.0 / WS).then_inc(s_silu, 1)

            def hi_part(act, j, n):
                wait(act, s_hh, j, 1, 1)
                if n >= 2:
                    wait(act, s_ht, j, 1, -1)
                act.activation(hs[n % 2][:, 0:F], hh[n % 2][:, :], ACT.Copy).then_inc(s_hi, 1)

            def weigh(act, j, n):
                wait(act, s_y, j, 1, 2)
                if n >= TR:
                    wait(act, s_add, j, 16, 16 - 16 * TR)
                act.activation(yo[n % TR][:, :], y_ps[:, :], ACT.Copy, scale=slot_w[:, bass.ds(j.value(), 1)])\
                    .then_inc(s_yo, 1)

            def step(act, j, n):
                gate_tile(act, j, n)
                hi_part(act, j, n)
                if n >= 1:
                    weigh(act, j.before(1), n - 1)

            act.wait_ge(s_tok, 3)
            tiles(act, step)
            weigh(act, At(None, 0, TILES - 1), TILES - 1)

        @block.vector
        def _(dve):
            dve.wait_ge(s_init, 1)
            dve.tensor_copy(bv_all[:, :], MA[:, 0:C]).then_inc(s_bias, 1)
            dve.tensor_copy(cols[:, 4 * CT + 2:4 * CT + 4], MA[:, C:C + 2]).then_inc(s_bias, 1)
            dve.wait_ge(s_tanh, 1)
            dve.tensor_scalar(bog_c, bo_c, tg_c[:, 0:1], None, ALU.mult).then_inc(s_bog, 1)
            dve.wait_ge(s_bog, 1)

            def attention(dve, g, guard):
                dve.sem_inc(g.c_free, 1)
                dve.sem_inc(g.on, 1)
                if not guard:
                    dve.memset(ok[:, :], 1.0).then_inc(g.ok, 1)

                def rest(b, m, n=1):
                    return res[:, bass.ds(b.value(CT * T, m * T), n * T)]

                def split_quarter(e, c):
                    wait(dve, s_wf[c % 2], e, 16 * 2, 16 * (c // 2 + 1), s_tanh)
                    wait(dve, s_wst[c % 2], e, 16 * 2, 16 * (c // 2), s_tanh)
                    dve.tensor_scalar(wp[c % 2][:, 0], wf[c % 2][:, :], WS, None, ALU.mult).then_inc(s_whi, 1)
                    wait(dve, s_whi, e, 4, c + 1)
                    dve.scalar_tensor_tensor(out=wp[c % 2][:, 1], in0=wf[c % 2][:, :], scalar=WS,
                                             in1=wp[c % 2][:, 0], op0=ALU.mult, op1=ALU.subtract).then_inc(s_wlo, 1)

                def slot(dve, t, par, a, b_, c):
                    bb, bc = t.before(1), t.before(2)
                    if b_ and guard:
                        wait(dve, g.turned, bb, 1)
                        for u in range(UM):
                            wait(dve, g.raw, bb, UM, u + 1)
                            dve.tensor_reduce(maxima[:, 2 * u:2 * u + 2],
                                              S[u % 2][:, :].rearrange("p (n t) -> p n t", n=2), AX_X, ALU.max)\
                                .then_inc(g.top, 1)
                        wait(dve, g.turned, bb, 1, 1)
                        wait(dve, g.shst, bb, 16)
                        dve.tensor_scalar(shift_t[:, :], O[0][0:H * TT, 0:P], -1.0 / SHIFT, None, ALU.mult)\
                            .then_inc(g.shift, 1)
                    if c:
                        for m in range(CT):
                            dve.tensor_scalar(rest(bc, m), rest(bc, m), bog_c[:, m:m + 1], None, ALU.add)\
                                .then_inc(g.xb, 1)
                    splits = [] if guard else quarters(t)
                    for v, e, n in splits:
                        if v == 0:
                            split_quarter(e, n)
                    if c:
                        wait(dve, g.zl, bc, 16 * GH, 16 * GH)
                        if not guard:
                            for n, (bound, op) in enumerate(((Z_LEAST, ALU.is_ge), (Z_MOST, ALU.is_le))):
                                wait(dve, g.ok, bc, 2, 1 + n)
                                dve.scalar_tensor_tensor(out=ok[:, :], in0=zl[:, :], scalar=bound,
                                                         in1=ok[:, :], op0=op, op1=ALU.mult).then_inc(g.ok, 1)
                        dve.reciprocal(zr[:, :], zl[:, :]).then_inc(g.rz, 1)
                    if a:
                        wait(dve, g.xc, t, 32, 32, s_tanh)
                        for m in range(CT):
                            dve.bn_stats(stats[:, m, :], rest(t, m)).then_inc(g.bst, 1)
                        for m in range(CT):
                            wait(dve, g.bst, t, CT, m + 1, s_tanh)
                            dve.bn_aggr(mv[:, m, :], stats[:, m, :]).then_inc(g.mv, 1)
                    for v in range(VS):
                        what = EXTRA.get(v)
                        for at, e, n in splits:
                            if at == v > 0:
                                split_quarter(e, n)
                        if a and v == 1:
                            wait(dve, g.rstd, t, 1, 1)
                            wait(dve, g.a_full, t, NA)
                            for m in range(CT):
                                dve.tensor_scalar(xn[:, m, :], rest(t, m), mv[:, m, 0:1], rstd[:, m:m + 1],
                                                  ALU.subtract, ALU.mult).then_inc(g.xn, 1)
                        if c and v == ON_AT:
                            wait(dve, g.oz, bc, 16 * 16, 16 * 16 + 16)
                            dve.tensor_tensor(on[:, :, :], oc[:, :, :], zc[:, :, :], ALU.mult).then_inc(g.on, 1)
                        if a and what in A_USES:
                            wait(dve, g.a_full, t, NA, A_USES[what] + 1)
                            m = int(what[1])
                            if what[0] in "qk":
                                f, bias, lo = (qf, bq_c, g.ql) if what[0] == "q" else (kf, bk_c, g.kl)
                                wait(dve, lo, t, 1)
                                dve.tensor_scalar(f[:, m, :], MA[:, :], bias[:, m:m + 1], None, ALU.add)\
                                    .then_inc(g.a_free, 1)
                                if m == CT - 1:
                                    parts, hi = (qs, g.qh) if what[0] == "q" else (ks, g.kh)
                                    wait(dve, g.qkst, t, 32)
                                    wait(dve, g.a_free, t, NA, A_USES[what] + 1)
                                    dve.tensor_copy(parts[:, 0], f[:, :, :]).then_inc(hi, 1)
                            else:
                                if m == 0:
                                    wait(dve, g.pv, t, VS, -VS)
                                for i in range(2):
                                    last = dve.tensor_tensor(
                                        V[par][:, 2 * m + i, :, 0:DK],
                                        MA[:, i * C:(i + 1) * C].rearrange("p (h c) -> p h c", h=H),
                                        bv_all[:, :].rearrange("p (h c) -> p h c", h=H), ALU.add)
                                last.then_inc(g.a_free, 1)
                        if c and what in C_USES:
                            wait(dve, g.c_full, bc, NCU, C_USES[what] + 1)
                            if what[0] == "o":
                                m = int(what[1])
                                wait(dve, g.xb, bc, CT, m + 1)
                                dve.scalar_tensor_tensor(out=rest(bc, m), in0=MC[:, :], scalar=tg_c[:, 0:1],
                                                         in1=rest(bc, m), op0=ALU.mult, op1=ALU.add).then_inc(g.c_free, 1)
                            elif what[0] == "t":
                                dve.tensor_copy(xT2[:, int(what[1]), :], MC[:, :]).then_inc(g.c_free, 1)
                            elif what == "lg":
                                dve.tensor_copy(lgT[:, :], MC[0:NE, 0:C]).then_inc(g.c_free, 1)
                            else:
                                dve.tensor_copy(logits[:, bass.ds(bc.value(CT * NE), CT * NE)], MC[:, 0:CT * NE])\
                                    .then_inc(g.c_free, 1)
                            if what == "o1":
                                for m in range(CT):
                                    wait(dve, g.c_free, bc, NCU, m + 2, s_tanh)
                                    dve.bn_stats(stats2[:, m, :], rest(bc, m)).then_inc(g.bst2, 1)
                                for m in range(CT):
                                    wait(dve, g.bst2, bc, CT, m + 1, s_tanh)
                                    dve.bn_aggr(mv2[:, m, :], stats2[:, m, :]).then_inc(g.mv2, 1)
                        if c and v == XN2_AT:
                            wait(dve, g.rstd2, bc, 1, 1)
                            wait(dve, g.xnst, bc, 16, 16)
                            for m in range(CT):
                                dve.tensor_scalar(xn2[:, m, :], rest(bc, m), mv2[:, m, 0:1], rstd2[:, m:m + 1],
                                                  ALU.subtract, ALU.mult).then_inc(g.xn2, 1)
                            wait(dve, g.xn2, bc, CT, CT)
                            dve.tensor_copy(xs2[:, 0], xn2[:, :, :]).then_inc(g.x2h, 1)
                        if b_ and v % TT == TT - 1:
                            g4 = v // TT
                            wait(dve, g.pv, bb, VS, v + 1)
                            wait(dve, g.oz, bb, 16 * 16, 16 - 16 * 16)
                            dve.tensor_copy(osum[1 - par][:, g4, :], O[g4 % 2][:, :]).then_inc(g.os, 1)

                slots(dve, slot)
                if not guard:
                    dve.wait_ge(g.ok, 2 * B + 1)
                    dve.tensor_reduce(ok_min[:, :], ok[:, :], AX_X, ALU.min)\
                        .then_inc(s_okall, 1)
                    dve.wait_ge(s_oksum, 1)
                    dve.tensor_scalar(bad[:, :], MC[:, 0:1], P - 0.5, None, ALU.is_lt).then_inc(s_bad, 1)
                dve.wait_ge(g.xnst, 16 * B + 16)

            both_runs(dve, attention)

            steps = [0]

            def done(ins):
                steps[0] += 1
                ins.then_inc(s_r, 1)
                return steps[0]

            def then(n):
                dve.wait_ge(s_r, n)

            dve.sem_inc(s_done, 1)
            dve.wait_ge(s_done, 2)
            for n in range(NT):
                last = done(dve.max(top8[:, n, :], logits[:, n * NE:(n + 1) * NE]))
            then(last)
            for n in range(NT):
                last = done(dve.max_index(idx8[:, n, :], top8[:, n, :], logits[:, n * NE:(n + 1) * NE]))
            dve.tensor_tensor(dl[:, :], top8[:, :, 1], top8[:, :, 0], ALU.subtract).then_inc(s_wexp, 1)
            then(last)
            last = done(dve.tensor_copy(idxf[:, :, :], idx8[:, :, 0:TOP].rearrange("p n k -> p k n")))
            then(last)
            dve.wait_ge(s_pool_c, 11)
            e_row = iota_f[:, 0:NE].unsqueeze(1).to_broadcast([P, NT, NE])
            for k in range(TOP):
                last = done(dve.tensor_tensor(onehot[:, k], e_row, idxf[:, k].unsqueeze(2).to_broadcast([P, NT, NE]),
                                              ALU.is_equal))
            then(last)
            ranks[0] = done(dve.tensor_tensor(picks[:, :, :], onehot[:, 0], onehot[:, 1], ALU.add))
            dve.wait_ge(s_wexp, 2)
            last = done(dve.tensor_scalar(el1[:, :], el[:, :], 1.0, None, ALU.add))
            then(last)
            last = done(dve.reciprocal(cw[:, 0], el1[:, :]))
            then(last)
            last = done(dve.tensor_tensor(cw[:, 1], cw[:, 0], el[:, :], ALU.mult))
            then(last)
            last = done(dve.tensor_scalar(cwg[:, :, :], cw[:, :, :], tg_c[:, 1:2], None, ALU.mult))
            then(last)
            last = done(dve.tensor_copy(w_hi[:, :], cwg[:, :, :].rearrange("p k n -> p (k n)")))
            then(last)
            last = done(dve.tensor_tensor(w_rest[:, :], cwg[:, :, :].rearrange("p k n -> p (k n)"), w_hi[:, :],
                                          ALU.subtract))
            then(last)
            last = done(dve.tensor_scalar(w_lo[:, :], w_rest[:, :], LO, None, ALU.mult))
            for n, sign in enumerate((-1.0, 1.0)):
                last = done(dve.tensor_scalar(spare[:, n:n + 1], tok_f[:, 0:1], float(TOK), sign, ALU.add, ALU.mult))
            dve.wait_ge(s_rank, 1)
            last = done(dve.tensor_copy(count_et[:, :].rearrange("p (e n) -> p e n", e=NE),
                                        MC[:, 0:NT * NE].rearrange("p (n e) -> p e n", e=NE)))
            then(last)
            last = done(dve.tensor_tensor_scan(upto_et[:, :], keep_et[:, :], count_et[:, :], 0.0, ALU.mult, ALU.add))
            then(last)
            last = done(dve.tensor_tensor(prev_et[:, :], upto_et[:, :], count_et[:, :], ALU.subtract))
            last = done(dve.tensor_scalar(tot_f[:, :], upto_et[:, NT - 1::NT], float(P - 1), None, ALU.add))
            then(last)
            last = done(dve.tensor_copy(tot_i[:, :], tot_f[:, :]))
            then(last)
            last = done(dve.tensor_scalar(ntl_i[:, :], tot_i[:, :], 7, None, ALU.logical_shift_right))
            then(last)
            last = done(dve.tensor_copy(ntl[:, :], ntl_i[:, :]))
            then(last)
            last = done(dve.tensor_tensor_scan(endt[:, :], ones[:, 0:NE], ntl[:, :], 0.0, ALU.mult, ALU.add))
            then(last)
            last = done(dve.tensor_tensor(startt[:, :], endt[:, :], ntl[:, :], ALU.subtract))
            then(last)
            last = done(dve.scalar_tensor_tensor(
                out=prev_et[:, :].rearrange("p (e n) -> p e n", e=NE),
                in0=startt[:, :].unsqueeze(2).to_broadcast([P, NE, NT]), scalar=float(P),
                in1=prev_et[:, :].rearrange("p (e n) -> p e n", e=NE), op0=ALU.mult, op1=ALU.add))
            then(last)
            last = done(dve.tensor_tensor(slot_e[:, :, :], MA[:, 0:NT * NE].rearrange("p (n e) -> p n e", e=NE),
                                          prev_et[:, :].rearrange("p (e n) -> p n e", e=NE), ALU.add))
            then(last)
            for k in range(TOP):
                last = done(dve.tensor_tensor(slot_m[:, k], onehot[:, k], slot_e[:, :, :], ALU.mult))
            then(last)
            last = done(dve.tensor_reduce(slot_f[:, :], slot_m[:, :, :, :].rearrange("p k n e -> p (k n) e"), AX_X,
                                          ALU.add))
            then(last)
            last = done(dve.tensor_copy(slot_i[:, :], slot_f[:, :]))
            then(last)
            last = done(dve.tensor_scalar(til_i[:, :], slot_i[:, :], 7, None, ALU.logical_shift_right))
            last = done(dve.tensor_scalar(row_i[:, :], slot_i[:, :], P - 1, None, ALU.bitwise_and))
            then(last)
            last = done(dve.tensor_copy(til_f[:, :], til_i[:, :]))
            last = done(dve.tensor_copy(row_f[:, :], row_i[:, :]))
            then(last)
            PAIRS = TOP * NT
            last = done(dve.tensor_tensor(til_tok[:, :, 0, :], iota_f[:, 0:TILES].unsqueeze(1).to_broadcast([P, PAIRS, TILES]),
                                          til_f[:, :].unsqueeze(2).to_broadcast([P, PAIRS, TILES]), ALU.is_equal))
            then(last)
            for n, values in enumerate((tok_f, w_hi, w_lo)):
                last = done(dve.tensor_tensor(til_tok[:, :, 1 + n, :], til_tok[:, :, 0, :],
                                              values[:, :].unsqueeze(2).to_broadcast([P, PAIRS, TILES]), ALU.mult))
            last = done(dve.tensor_tensor(row_hot[:, :, :], iota_f[:, :].unsqueeze(1).to_broadcast([P, PAIRS, P]),
                                          row_f[:, :].unsqueeze(2).to_broadcast([P, PAIRS, P]), ALU.is_equal))
            hots[0] = last
            last = done(dve.tensor_tensor(le[:, :, :], endt[:, :].unsqueeze(1).to_broadcast([P, TILES, NE]),
                                          iota_f[:, 0:TILES].unsqueeze(2).to_broadcast([P, TILES, NE]), ALU.is_le))
            then(last)
            last = done(dve.tensor_reduce(et_f[:, :], le[:, :, :], AX_X, ALU.add))
            then(last)
            last = done(dve.tensor_scalar(et_f[:, :], et_f[:, :], float(NE - 1), None, ALU.min))
            then(last)
            last = done(dve.tensor_copy(et_i[:, :], et_f[:, :]))
            last = done(dve.tensor_scalar(table[:, 0:TILES], et_f[:, :], 1.0, 16.0, ALU.add, ALU.mult))
            last = done(dve.tensor_scalar(table[:, 2 * TILES:2 * TILES + NE], endt[:, :], 1.0, None, ALU.add))
            then(last)
            last = done(dve.tensor_scalar(eb_i[:, :], et_i[:, :], EB - 1, None, ALU.bitwise_and))
            then(last)
            last = done(dve.tensor_copy(et_f[:, :], eb_i[:, :]))
            then(last)
            dve.tensor_scalar(table[:, TILES:2 * TILES], et_f[:, :], float(2 * WCOL), None, ALU.mult).then_inc(s_table, 1)
            dve.wait_ge(s_tab, 1)
            tab = MC[:, 0:4 * TILES].rearrange("p (k n) -> p k n", k=4)
            dve.tensor_copy(slot_tok[:, :], tab[:, 1]).then_inc(s_tok, 1)
            last = done(dve.tensor_scalar(slot_pad[:, :], tab[:, 0], spare[:, 0:1], spare[:, 1:2], ALU.mult, ALU.add))
            last = done(dve.tensor_scalar(slot_w[:, :], tab[:, 3], 1.0 / (LO * WS * HS), None, ALU.mult))
            then(last)
            dve.tensor_tensor(slot_out[:, :], tab[:, 1], slot_pad[:, :], ALU.add).then_inc(s_tok, 1)
            dve.scalar_tensor_tensor(out=slot_w[:, :], in0=tab[:, 2], scalar=1.0 / (WS * HS), in1=slot_w[:, :],
                                     op0=ALU.mult, op1=ALU.add).then_inc(s_tok, 1)

            def x_out(dve, j, n):
                wait(dve, s_xt, j, 1, 1)
                if n >= 2:
                    wait(dve, s_h, j, 1, -1)
                dve.tensor_copy(xT[n % 2][:, :, :], xt_ps.rearrange("p (k n) -> p k n", n=P)).then_inc(s_xT, 1)

            def step(dve, j, n):
                par = n % 2
                wait(dve, s_silu, j, 1, 1)
                if n >= 1:
                    wait(dve, s_ht, j, 1, -1)
                dve.scalar_tensor_tensor(out=hh[par][:, :], in0=h3_ps, scalar=HS / WS, in1=act1[par][:, :],
                                         op0=ALU.mult, op1=ALU.mult).then_inc(s_hh, 1)
                if n < TILES - 1:
                    x_out(dve, At(j.i, j.mul, j.add + 1), n + 1)
                wait(dve, s_hi, j, 1, 1)
                dve.tensor_tensor(hs[par][:, F:2 * F], hh[par][:, :], hs[par][:, 0:F], ALU.subtract).then_inc(s_lo, 1)
                wait(dve, s_ht, j, 1, 1)
                if n >= 2:
                    wait(dve, s_y, j, 1)
                dve.tensor_copy(hT[par][:, 0:2 * (FT - 1), :],
                                ht_ps[:, 0:2 * (FT - 1) * P].rearrange("p (k n) -> p k n", n=P)).then_inc(s_hT, 1)
                dve.tensor_copy(hT[par][0:FL, 2 * (FT - 1):2 * FT, :],
                                ht_ps[0:FL, 2 * (FT - 1) * P:2 * FT * P].rearrange("p (k n) -> p k n", n=P))\
                    .then_inc(s_hT, 1)

            x_out(dve, At(None, 0, 0), 0)
            tiles(dve, step)

        @block.tensor
        def _(pe):
            pe.wait_ge(s_const, 16 * NCONST)
            pe.wait_ge(s_pool_c, 5)
            pe.matmul(MA[:, 0:C], ones[0:1, :], bv_r, start=True, stop=True)
            pe.matmul(MA[:, C:C + 2], ones[0:1, :], g_r, start=True, stop=True).then_inc(s_init, 1)
            pe.wait_ge(s_bias, 2)

            def attention(pe, g, guard):
                def scores(b, par, v):
                    g4, st = divmod(v, TT)
                    if v == 0:
                        wait(pe, g.qk, b, 16 * 4 * PARTS, 16 * 4 * PARTS)
                    for n in range(2):
                        u = 2 * v + n
                        wait(pe, g.exp, b, 2 * VS, u - 1)
                        for s in range(2):
                            r0 = 64 * s
                            last = pe.matmul(S[u % 2][:, s * T:(s + 1) * T],
                                             K[par][r0:r0 + PARTS * DK + 1, 2 * g4 + n, st * P:(st + 1) * P],
                                             Q[par][r0:r0 + PARTS * DK + 1, 2 * g4 + n, :], start=True, stop=True)
                        last.then_inc(g.full, 1)

                def row_maxima(b, par):
                    wait(pe, g.qk, b, 16 * 4 * PARTS, 16 * 4 * PARTS)
                    wait(pe, g.exp, b, 2 * VS)
                    for u in range(UM):
                        h = u // (TT // 2)
                        r0 = 64 * (h % 2)
                        wait(pe, g.top, b, UM, u - 1)
                        for n in range(2):
                            tt = 2 * (u % (TT // 2)) + n
                            last = pe.matmul(S[u % 2][:, n * T:(n + 1) * T],
                                             Q[par][r0:r0 + PARTS * DK, h // 2, tt * P:(tt + 1) * P],
                                             K[par][r0:r0 + PARTS * DK, h // 2, :], start=True, stop=True)
                        last.then_inc(g.raw, 1)
                    wait(pe, g.top, b, UM, UM)
                    wait(pe, g.os, b, GROUPS, 0, s_bias)
                    pe.transpose(O[0][0:H * TT, 0:P], maxima[:, :], ident[:, :]).then_inc(g.turned, 1)
                    wait(pe, g.shld, b, 32, 32)

                def values(b, par, v):
                    g4, st = divmod(v, TT)
                    if v == 0:
                        wait(pe, g.a_free, b, NA, A_USES["v1"] + 1)
                        pe.wait_ge(s_vone, 3)
                    wait(pe, g.exp, b, 2 * VS, 2 * v + 2)
                    if st == 0:
                        wait(pe, g.os, b, GROUPS, g4 - 1)
                    for j in range(GH):
                        u = 2 * v + j // 2
                        last = pe.matmul(O[g4 % 2][2 * DK * j:2 * DK * (j + 1), :], V[par][:, st, GH * g4 + j, :],
                                         prob[:, u % RING, (j % 2) * T:(j % 2 + 1) * T],
                                         start=(st == 0), stop=(st == TT - 1), tile_position=(0, 2 * DK * j))
                    last.then_inc(g.pv, 1)

                def project(t, par, what):
                    m = int(what[1])
                    wait(pe, g.a_free, t, NA, A_USES[what])
                    if what[0] == "v":
                        for i in range(2):
                            st = 2 * m + i
                            for k in range(CT):
                                last = pe.matmul(MA[:, i * C:(i + 1) * C], ctx_sb[par][:, k, st * P:(st + 1) * P],
                                                 wv[:, k, :], start=(k == 0), stop=(k == CT - 1))
                    else:
                        if what == "k0":
                            wait(pe, g.xc, t, 32, 32)
                        if what == "q0":
                            wait(pe, g.xn, t, CT, CT)
                        w, src = (wq, xn) if what[0] == "q" else (wk, ctx_sb[par])
                        for k in range(CT):
                            last = pe.matmul(MA[:, :], w[:, k, m * P:(m + 1) * P], src[:, k, :],
                                             start=(k == 0), stop=(k == CT - 1))
                    last.then_inc(g.a_full, 1)

                def output(b, what):
                    wait(pe, g.c_free, b, NCU, C_USES[what] + 1, s_bias if what == "lt" else None)
                    if what[0] == "o":
                        m = int(what[1])
                        if m == 0:
                            wait(pe, g.on, b, 1, 2)
                        for k in range(CT):
                            last = pe.matmul(MC[:, :], wo[:, k, m * P:(m + 1) * P], on[:, k, :],
                                             start=(k == 0), stop=(k == CT - 1))
                    elif what[0] == "t":
                        m = int(what[1])
                        wait(pe, g.xn2, b, CT, m + 1)
                        for k in range(TT):
                            last = pe.transpose(MC[:, k * P:(k + 1) * P], xn2[:, m, k * P:(k + 1) * P], ident[:, :])
                    elif what == "lt":
                        for m in range(CT):
                            last = pe.transpose(MC[:, m * NE:(m + 1) * NE], lgT[:, m * P:(m + 1) * P],
                                                ident[0:NE, 0:NE])
                    else:
                        for k in range(TT):
                            last = pe.matmul(MC[0:NE, 0:C], gate[:, k, :], xT2[:, :, k * P:(k + 1) * P],
                                             start=(k == 0), stop=(k == TT - 1))
                    last.then_inc(g.c_full, 1)

                def slot(pe, t, par, a, b_, c):
                    bb, bc = t.before(1), t.before(2)
                    first = t.i is None and t.add == 1
                    last_b = t.i is None and t.add == B
                    if b_ and guard:
                        row_maxima(bb, 1 - par)
                    if b_ and (first or guard):
                        scores(bb, 1 - par, 0)
                    for v in range(VS):
                        if b_ and v + 1 < VS:
                            scores(bb, 1 - par, v + 1)
                        what = EXTRA.get(v)
                        if a and what in A_USES:
                            project(t, par, what)
                        if c and what in C_USES:
                            output(bc, what)
                        if b_:
                            if v == VS - 1 and not last_b and not guard:
                                scores(t, par, 0)
                            values(bb, 1 - par, v)

                slots(pe, slot)
                pe.wait_ge(g.c_free, NCU * B + 1)
                if not guard:
                    pe.wait_ge(s_okall, 1)
                    pe.matmul(MC[:, 0:1], ones[:, :], ok_min[:, :], start=True, stop=True).then_inc(s_oksum, 1)
                pe.wait_ge(g.os, GROUPS * B)

            both_runs(pe, attention)

            pe.sem_inc(s_done, 1)
            pe.wait_ge(s_r, ranks[0])
            pe.matmul(MA[:, 0:NT * NE], below[:, :], picks[:, :, :].rearrange("p n e -> p (n e)"), start=True, stop=True)
            pe.matmul(MC[:, 0:NT * NE], ones[:, :], picks[:, :, :].rearrange("p n e -> p (n e)"), start=True, stop=True)\
                .then_inc(s_rank, 1)
            pe.wait_ge(s_r, hots[0])
            for n in range(TOP * NT):
                last = pe.matmul(MC[:, 0:4 * TILES], row_hot[:, n, :],
                                 til_tok[:, n, :, :].rearrange("p k n -> p (k n)"), start=(n == 0),
                                 stop=(n == TOP * NT - 1))
            last.then_inc(s_tab, 1)
            pe.wait_ge(s_table, 1)
            pe.sem_inc(s_y, 1)

            def turn_x(j, n):
                pe.wait_ge(s_xg[n % TR], At(j.i, j.mul // TR, j.add // TR).value(16, 16))
                wait(pe, s_xT, j, 1)
                for k in range(2 * TT):
                    last = pe.transpose(xt_ps[:, k * P:(k + 1) * P], xg[n % TR][:, k * P:(k + 1) * P], ident16[:, :])
                last.then_inc(s_xt, 1)

            def weights_of(j):
                landed = pe.value_load(table[0:1, bass.ds(j.value(), 1)], min_val=16, max_val=16 * NE)
                return landed, ((landed - 16) & (16 * (EB - 1))) * (2 * WCOL // 16)

            def hidden(j, par, off):
                for k in range(TT):
                    for xp, wp_ in ((0, 0), (0, 1), (1, 0)):
                        for n, ps in enumerate((h1_ps, h3_ps)):
                            last = pe.matmul(ps, xT[par][:, xp * TT + k, :],
                                             W[:, bass.ds(off + (wp_ * WCOL + (2 * k + n) * F), F)],
                                             start=(k == 0 and (xp, wp_) == (0, 0)),
                                             stop=(k == TT - 1 and (xp, wp_) == (1, 0)))
                last.then_inc(s_h, 1)

            def turn_h(j, par):
                wait(pe, s_lo, j, 1, 1)
                wait(pe, s_hT, j, 2)
                for k in range(FT):
                    n = P if k < FT - 1 else FL
                    for part in range(2):
                        c = part * F + k * P
                        last = pe.transpose(ht_ps[0:n, (2 * k + part) * P:(2 * k + part + 1) * P], hs[par][:, c:c + n],
                                            ident16[:, :])
                last.then_inc(s_ht, 1)

            def down(j, par, off):
                wait(pe, s_hT, j, 2, 2)
                wait(pe, s_yo, j, 1)
                for k in range(FT):
                    n = P if k < FT - 1 else FL
                    for hp, wp_ in ((0, 0), (0, 1), (1, 0)):
                        last = pe.matmul(y_ps[:, :], hT[par][0:n, 2 * k + hp, :],
                                         W[0:n, bass.ds(off + (wp_ * WCOL + W2 + k * T), T)],
                                         start=(k == 0 and (hp, wp_) == (0, 0)),
                                         stop=(k == FT - 1 and (hp, wp_) == (1, 0)))
                last.then_inc(s_y, 1)

            def step(pe, j, n):
                if n >= 1:
                    _, off_before = weights_of(j.before(1))
                landed, off = weights_of(j)
                pe.wait_ge(s_wr, landed)
                wait(pe, s_xT, j, 1, 1)
                if n >= 1:
                    turn_h(j.before(1), (n - 1) % 2)
                hidden(j, n % 2, off)
                if n < TILES - 1:
                    turn_x(At(j.i, j.mul, j.add + 1), n + 1)
                if n >= 1:
                    down(j.before(1), (n - 1) % 2, off_before)

            turn_x(At(None, 0, 0), 0)
            tiles(pe, step)
            turn_h(At(None, 0, TILES - 1), (TILES - 1) % 2)
            down(At(None, 0, TILES - 1), (TILES - 1) % 2, weights_of(At(None, 0, TILES - 1))[1])


def kernel(**inputs):
    import numpy as np
    import concourse.bacc as bacc
    from concourse.bass_utils import run_bass_kernel_spmd

    a = {k: np.asarray(v) for k, v in inputs.items()}
    w1, w3, w2 = a["L0_ffn_w1"], a["L0_ffn_w3"], a["L0_ffn_w2"]
    NE, F, T = w1.shape
    FT = -(-F // P)
    w13 = np.concatenate([w1, w3], axis=1).transpose(0, 2, 1).reshape(NE, T // P, P, 2 * F)
    w2T = np.zeros((NE, FT * P, T), w2.dtype)
    w2T[:, :F] = w2.transpose(0, 2, 1)
    wall = np.concatenate([w13.transpose(0, 2, 1, 3).reshape(NE, P, -1),
                           w2T.reshape(NE, FT, P, T).transpose(0, 2, 1, 3).reshape(NE, P, -1)], axis=2)
    arrays = {
        "x": a["x"], "ctx_in": a["ctx_2048"], "g_xattn": a["g_xattn"], "g_ffn": a["g_ffn"],
        "WqT": a["L0_xattn_Wq"].T, "bq": a["L0_xattn_bq"], "WkT": a["L0_xattn_Wk"].T, "bk": a["L0_xattn_bk"],
        "WvT": a["L0_xattn_Wv"].T, "bv": a["L0_xattn_bv"], "WoT": a["L0_xattn_Wo"].T, "bo": a["L0_xattn_bo"],
        "gateT": a["L0_ffn_gate_w"].T,
        "wall": wall,
    }
    for k in ("bq", "bk", "bo"):
        arrays[k] = arrays[k].reshape(-1, P).T
    arrays = {k: np.ascontiguousarray(v) for k, v in arrays.items()}
    nc = bacc.Bacc("TRN2", target_bir_lowering=False, num_devices=1)
    args = [nc.dram_tensor(k, v.shape, mybir.dt.from_np(v.dtype), kind="ExternalInput").ap()
            for k, v in arrays.items()]
    B, C, T = a["x"].shape
    out = nc.dram_tensor("out", [B * C + P, T], F32, kind="ExternalOutput").ap()
    flamingo_kernel(nc, *args, out)
    r = run_bass_kernel_spmd(nc, [arrays], core_ids=[0])
    return r.results[0]["out"][:B * C].reshape(B, C, T)
```

```python
from contextlib import ExitStack

import concourse.bass as bass
from concourse import mybir

ALU = mybir.AluOpType
ACT = mybir.ActivationFunctionType
AX_X = mybir.AxisListType.X
F32 = mybir.dt.float32
F16 = mybir.dt.float16
I32 = mybir.dt.int32
U32 = mybir.dt.uint32
U16 = mybir.dt.uint16

P = 128
EPS = 1e-5


class At:

    def __init__(self, i, mul, add):
        self.i, self.mul, self.add = i, mul, add

    def value(self, k=1, c=0):
        if self.i is None:
            return k * self.add + c
        return self.i * (k * self.mul) + (k * self.add + c)

    def before(self, n):
        return At(self.i, self.mul, self.add - n)


def wait(eng, sem, at, k, c=0, alone=None):
    if at.i is None and k * at.add + c <= 0:
        return
    assert k * at.add + c > 0, "a wait against nothing in a loop's first round"
    value = at.value(k, c)
    if alone is not None and at.i is not None:
        value = eng.to_reg(value)
        eng.wait_ge(alone, 1)
    eng.wait_ge(sem, value)


class Signals:

    def __init__(self, sem):
        self.xc = sem("xc")
        self.bst, self.mv, self.veps, self.rstd, self.xn = sem("bst"), sem("mv"), sem("veps"), sem("rstd"), sem("xn")
        self.bst2, self.mv2, self.veps2, self.rstd2, self.xn2 = (
            sem("bst2"), sem("mv2"), sem("veps2"), sem("rstd2"), sem("xn2"))
        self.ch, self.cl, self.xh, self.xl = sem("ch"), sem("cl"), sem("xh"), sem("xl")
        self.oh, self.ol = sem("oh"), sem("ol")
        self.a_full, self.a_free = sem("a_full"), sem("a_free")
        self.c_full = sem("c_full")
        self.c_free = sem("c_free")
        self.qh, self.ql, self.kh, self.kl = sem("qh"), sem("ql"), sem("kh"), sem("kl")
        self.qkst = sem("qkst")
        self.qk = sem("qk")
        self.full = sem("full")
        self.exp = sem("exp")
        self.pv = sem("pv")
        self.os = sem("os")
        self.zl = sem("zl")
        self.rz = sem("rz")
        self.zst = sem("zst")
        self.oz = sem("oz")
        self.on = sem("on")
        self.xb = sem("xb")
        self.outst = sem("outst")
        self.x2h, self.x2l = sem("x2h"), sem("x2l")
        self.xnst = sem("xnst")
        self.best = sem("best")
        self.ok = sem("ok")
        self.raw = sem("raw")
        self.top = sem("top")
        self.turned = sem("turned")
        self.shift = sem("shift")
        self.shst = sem("shst")
        self.shld = sem("shld")


def flamingo_kernel(nc, x, ctx_in, g_xattn, g_ffn, WqT, bq, WkT, bk, WvT, bv, WoT, bo, gateT, wall, out):
    B, C, T = x.shape
    H, DK = 16, C // 16
    CT, TT = C // P, T // P
    NE = gateT.shape[1]
    WCOL = wall.shape[2]
    FT = 3
    F = (WCOL - FT * T) // (2 * TT)
    assert -(-F // P) == FT
    FL = F - (FT - 1) * P
    TOP = 2
    TOK = B * C
    NT = TOK // P
    TILES = (TOP * TOK + NE * (P - 1)) // P
    SCALE = DK ** -0.5
    ZW = H * T // P
    G = H // 2
    SHIFT = 64.0
    PARTS = 3
    GROUPS, GH = H // 4, 4
    RING = 4
    UM = H * TT // 2
    Z_LEAST, Z_MOST = 1e-20, 1e30
    HOT = TOP * NT // 4
    LO = 2048.0
    TR = 4
    EB = 4
    HB = 2 * (FT - 1) + 1
    assert 2 * FL == P
    W2 = TT * 2 * F
    WS, HS = 256.0, 16.0
    WQ = WCOL // 4

    q_dram = nc.dram_tensor("q_parts", [2, C, T], F16).ap()
    k_dram = nc.dram_tensor("k_parts", [2, C, T], F16).ap()
    z_dram = nc.dram_tensor("inverse_sums", [GH, GROUPS, T], F32).ap()
    shift_dram = nc.dram_tensor("shift_rows", [H, T], F16).ap()
    xn_dram = nc.dram_tensor("tokens_normed", [TOK, 2 * T], F16).ap()
    w_dram = nc.dram_tensor("weight_parts", [NE, P, 2, WCOL], F16).ap()

    x_v = x.rearrange("b (m p) t -> b p m t", p=P)
    c_v = ctx_in.rearrange("b (m p) t -> b p m t", p=P)
    out_v = out[0:TOK].rearrange("(b m p) t -> b p m t", b=B, p=P)

    top = ExitStack()
    with top:
        def sb(name, shape, dt=F32, stack=top):
            return stack.enter_context(nc.sbuf_tensor(name, shape, dt))

        def sem(name):
            return top.enter_context(nc.semaphore(name))

        res = sb("residual", [P, NT * T])
        ident = sb("ident", [P, P])
        ident16 = sb("ident16", [P, P], F16)
        ones = sb("ones", [P, P])
        below = sb("below", [P, P])
        gate = sb("gate", [P, TT, NE])
        lgT = sb("lgT", [NE, C])
        logits = sb("logits", [P, NT * NE])
        rows = sb("rows", [1, 2 * C + 2])
        cols = sb("cols", [P, 4 * CT + 5])
        ok = sb("ok", [P, ZW])
        ok_min = sb("ok_min", [P, 1])
        bad = sb("bad", [P, 1], U16)
        maxima = sb("maxima", [P, H * TT])
        shift_t = sb("shift_t", [H * TT, P], F16)
        neg_half = sb("neg_half", [P, CT])

        wf = [sb(f"wf{i}", [P, WQ], F32) for i in range(2)]
        wp = [sb(f"wp{i}", [P, 2, WQ], F16) for i in range(2)]
        top8 = sb("top8", [P, NT, 8])
        idx8 = sb("idx8", [P, NT, 8], U32)
        iota_i = sb("iota_i", [P, P], I32)
        iota_f = sb("iota_f", [P, P])
        tok_i = sb("tok_i", [P, TOP * NT], I32)
        tok_f = sb("tok_f", [P, TOP * NT])
        keep_et = sb("keep_et", [P, NE * NT])

        att = ExitStack()
        Q = [sb(f"Q{i}", [P, G, T], F16, att) for i in range(2)]
        K = [sb(f"K{i}", [P, G, T], F16, att) for i in range(2)]
        V = [sb(f"V{i}", [P, TT, H, 2 * DK], F32, att) for i in range(2)]
        prob = sb("prob", [P, RING, 2 * T], F32, att)
        ctx_sb = [sb(f"ctx{i}", [P, CT, T], F32, att) for i in range(2)]
        xn = sb("xn", [P, CT, T], F32, att)
        qf = sb("qf", [P, CT, T], F32, att)
        kf = sb("kf", [P, CT, T], F32, att)
        qs = sb("qs", [P, 2, CT, T], F16, att)
        ks = sb("ks", [P, 2, CT, T], F16, att)
        osum = [sb(f"osum{i}", [P, GROUPS, T], F32, att) for i in range(2)]
        ocz = sb("ocz", [P, 2, CT, T], F32, att)
        oc, zc = ocz[:, 0], ocz[:, 1]
        w4 = ocz[:, :, :, :].rearrange("p a b t -> p (a b t)").rearrange("p (n k c) -> p n k c", n=4, k=CT)
        zl = sb("zl", [P, ZW], F32, att)
        zr = sb("zr", [P, ZW], F32, att)
        on = kf
        xn2 = sb("xn2", [P, CT, T], F32, att)
        xs2 = sb("xs2", [P, 2, CT, T], F16, att)
        xT2 = sb("xT2", [P, CT, T], F32, att)
        w4s = sb("w4s", [P, 2, 4, CT, C], F16, att)
        cs = sb("cs", [P, 2, CT, T], F16, att)
        xs = sb("xs", [P, 2, CT, T], F16, att)
        os_ = sb("os", [P, 2, CT, T], F16, att)
        bv_all = sb("bv_all", [P, C], F32, att)
        stats = sb("stats", [P, CT, 6], F32, att)
        mv = sb("mv", [P, CT, 2], F32, att)
        veps = sb("veps", [P, CT], F32, att)
        rstd = sb("rstd", [P, CT], F32, att)
        stats2 = sb("stats2", [P, CT, 6], F32, att)
        mv2 = sb("mv2", [P, CT, 2], F32, att)
        veps2 = sb("veps2", [P, CT], F32, att)
        rstd2 = sb("rstd2", [P, CT], F32, att)
        att.close()

        W = sb("W", [P, EB * 2 * WCOL], F16)
        warm = sb("warm", [P, 1])
        idxf = sb("idxf", [P, TOP, NT])
        dl = sb("dl", [P, NT])
        el = sb("el", [P, NT])
        el1 = sb("el1", [P, NT])
        cw = sb("cw", [P, TOP, NT])
        cwg = sb("cwg", [P, TOP, NT])
        onehot = sb("onehot", [P, TOP, NT, NE])
        picks = sb("picks", [P, NT, NE])
        count_et = sb("count_et", [P, NE * NT])
        upto_et = sb("upto_et", [P, NE * NT])
        prev_et = sb("prev_et", [P, NE * NT])
        tot_f = sb("tot_f", [P, NE])
        tot_i = sb("tot_i", [P, NE], I32)
        ntl_i = sb("ntl_i", [P, NE], I32)
        ntl = sb("ntl", [P, NE])
        endt = sb("endt", [P, NE])
        startt = sb("startt", [P, NE])
        slot_e = sb("slot_e", [P, NT, NE])
        slot_m = sb("slot_m", [P, TOP, NT, NE])
        slot_f = sb("slot_f", [P, TOP * NT])
        slot_i = sb("slot_i", [P, TOP * NT], I32)
        til_i = sb("til_i", [P, TOP * NT], I32)
        row_i = sb("row_i", [P, TOP * NT], I32)
        til_f = sb("til_f", [P, TOP * NT])
        row_f = sb("row_f", [P, TOP * NT])
        row_hot = sb("row_hot", [P, TOP * NT, P], F16)
        til_tok = sb("til_tok", [P, TOP * NT, 2, TILES], F16)
        til_w = sb("til_w", [P, TOP * NT, 2, TILES], F16)
        w_hi = sb("w_hi", [P, TOP * NT], F16)
        w_rest = sb("w_rest", [P, TOP * NT])
        w_lo = sb("w_lo", [P, TOP * NT], F16)
        slot_tok = sb("slot_tok", [P, TILES], U32)
        slot_out = sb("slot_out", [P, TILES], U32)
        slot_w = sb("slot_w", [P, TILES])
        slot_pad = sb("slot_pad", [P, TILES])
        spare = sb("spare", [P, 2])
        le = sb("le", [P, TILES, NE])
        et_f = sb("et_f", [P, TILES])
        table = sb("table", [P, TILES + NE], U16)
        xg = [sb(f"xg{i}", [P, 2 * T], F16) for i in range(TR)]
        xT = [sb(f"xT{i}", [P, 2 * TT, P], F16) for i in range(2)]
        act1 = [sb(f"act1_{i}", [P, F]) for i in range(2)]
        hh = [sb(f"hh{i}", [P, F]) for i in range(2)]
        hs = [sb(f"hs{i}", [P, 2 * F], F16) for i in range(2)]
        hT = [sb(f"hT{i}", [P, HB, P], F16) for i in range(2)]
        yo = [sb(f"yo{i}", [P, T]) for i in range(TR)]

        S = [top.enter_context(nc.psum_tensor(f"S{i}", [P, 2 * T], F32)) for i in range(2)]
        O = [top.enter_context(nc.psum_tensor(f"O{i}", [P, T], F32)) for i in range(2)]
        MA = top.enter_context(nc.psum_tensor("MA", [P, T], F32))
        MC = top.enter_context(nc.psum_tensor("MC", [P, T], F32))
        h1_ps, h3_ps = S[0][:, 0:F], S[0][:, T:T + F]
        xt_ps, ht_ps = S[1][:, 0:T].bitcast(F16), S[1][:, T:2 * T].bitcast(F16)
        y_ps = O[0]

        bq_c, bk_c, bo_c = (cols[:, n * CT:(n + 1) * CT] for n in range(3))
        bog_c = cols[:, 3 * CT:4 * CT]
        tg_c = cols[:, 4 * CT:4 * CT + 2]
        tgs_c = cols[:, 4 * CT + 4:4 * CT + 5]
        bv_r = rows[:, 0:C]
        g_r = rows[:, 2 * C:2 * C + 2]

        fast = Signals(lambda name: sem("f_" + name))
        slow = Signals(lambda name: sem("g_" + name))
        s_okall = sem("s_okall")
        s_oksum = sem("s_oksum")
        s_bad = sem("s_bad")
        s_rows = [sem(f"s_rows{i}") for i in range(2)]
        s_done = sem("s_done")

        def both_runs(eng, attention):
            attention(eng, fast, False)
            eng.wait_ge(s_bad, 1)
            with eng.If(eng.value_load(bad[0:1, 0:1], min_val=0, max_val=1) > 0):
                attention(eng, slow, True)

        NCONST2 = 3 + 3 + 1
        s_rowc = sem("s_rowc")
        s_const = sem("s_const")
        s_const2 = sem("s_const2")
        s_pool_c = sem("s_pool_c")
        s_num = sem("s_num")
        s_best = sem("s_best")
        s_hot = sem("s_hot")
        s_tilw = sem("s_tilw")
        s_w4 = sem("s_w4")
        s_init = sem("s_init")
        s_bias = sem("s_bias")
        s_tanh = sem("s_tanh")
        s_bog = sem("s_bog")
        s_vone = sem("s_vone")
        A_USES = {n: k for k, n in enumerate(("k0", "k1", "q0", "q1", "v0", "v1"))}
        C_USES = {n: k for k, n in enumerate(("o0", "o1", "t0", "t1", "lg", "lt"))}
        NA, NCU = len(A_USES), len(C_USES)
        EXTRA = {3: "k0", 4: "k1", 5: "q0", 7: "q1", 8: "o0", 9: "v0", 10: "o1", 11: "v1", 12: "t0", 13: "t1",
                 14: "lg", 15: "lt"}
        ON_AT, XN2_AT, SPLIT_AT = 6, 11, 6
        OZ = 16 * 4 * GH
        VS = GROUPS * TT

        def quarters(t):
            if t.i is None and t.add == 0:
                steps, experts = (4, 8, 11, 12), (0,)
            elif t.i is None and t.add == 1:
                steps, experts = (0, 2, 4, 6, 8, 10, 12, 14), (1, 2)
            elif t.i is None and t.add == B:
                steps, experts = (0, 2, 4, 6, 8, 10, 12, 13), (NE - 3, NE - 2)
            elif t.i is None and t.add == B + 1:
                steps, experts = (7, 7), (NE - 1,)
            else:
                steps, experts = (0, 5, 9, 12), (t.before(-1),)
            experts = [e if isinstance(e, At) else At(None, 0, e) for e in experts]
            return [(v, experts[n // 4], n % 4) for n, v in enumerate(steps)]

        def slots(eng, slot):
            slot(eng, At(None, 0, 0), 0, True, False, False)
            slot(eng, At(None, 0, 1), 1, True, True, False)
            with eng.Fori(0, (B - 2) // 2) as i:
                slot(eng, At(i, 2, 2), 0, True, True, True)
                slot(eng, At(i, 2, 3), 1, True, True, True)
            slot(eng, At(None, 0, B), 0, False, True, True)
            slot(eng, At(None, 0, B + 1), 1, False, False, True)

        s_r = sem("s_r")
        s_wexp = sem("s_wexp")
        s_rank = sem("s_rank")
        s_tab = sem("s_tab")
        s_tok = sem("s_tok")
        s_table = sem("s_table")
        s_wr = sem("s_wr")
        s_wf = [sem(f"s_wf{i}") for i in range(2)]
        s_whi, s_wlo = sem("s_whi"), sem("s_wlo")
        s_wst = [sem(f"s_wst{i}") for i in range(2)]
        s_hi = sem("s_hi")
        s_lo = sem("s_lo")
        s_xg = [sem(f"s_xg{i}") for i in range(TR)]
        s_xt = sem("s_xt")
        s_xT = sem("s_xT")
        s_h1 = sem("s_h1")
        s_h = sem("s_h")
        s_silu = sem("s_silu")
        s_hh = sem("s_hh")
        s_ht = sem("s_ht")
        s_hT = sem("s_hT")
        s_y = sem("s_y")
        s_yo = sem("s_yo")

        def tiles(eng, step):
            first = TR - 1
            rounds = (TILES - first - 1) // TR
            for n in range(first):
                step(eng, At(None, 0, n), n)
            with eng.Fori(0, rounds) as i:
                for n in range(first, first + TR):
                    step(eng, At(i, TR, n), n)
            for n in range(first + rounds * TR, TILES):
                step(eng, At(None, 0, n), n)


        s_add = sem("s_add")
        s_stored = sem("s_stored")
        s_spare = sem("s_spare")

        ranks, hots = [0], []

        block = top.enter_context(nc.Block())

        @block.sync
        def _(sp):
            sp.dma_start(w4[:, 0, :, :], WkT.rearrange("(k p) n -> p k n", p=P)).then_inc(s_const, 16)

            def attention(sp, g, guard):
                sp.sem_inc(g.oz, 16)
                sp.sem_inc(g.xnst, 16)

                def load_batch(b, par):
                    sp.dma_start(ctx_sb[par][:, :, :],
                                 c_v[bass.ds(b.value(), 1)].rearrange("b p m t -> p (b m) t")).then_inc(g.xc, 16)
                    sp.dma_start(res[:, bass.ds(b.value(CT * T), CT * T)].rearrange("p (m t) -> p m t", m=CT),
                                 x_v[bass.ds(b.value(), 1)].rearrange("b p m t -> p (b m) t")).then_inc(g.xc, 16)

                def slot(sp, t, par, a, b_, c):
                    if b_ and guard:
                        bb = t.before(1)
                        wait(sp, g.shld, bb, 32, 0, s_bog)
                        wait(sp, g.shift, bb, 1, 1, s_bog)
                        sp.dma_start(shift_dram.rearrange("h (n p) -> (h n) p", p=P), shift_t[:, :])\
                            .then_inc(g.shst, 16)
                        wait(sp, g.shst, bb, 16, 16, s_bog)
                        for s in range(2):
                            row = 64 * s + PARTS * DK
                            sp.dma_start(Q[1 - par][row:row + 1, :, :],
                                         shift_dram.rearrange("(a g s) t -> s a g t", s=2, a=1)[s]).then_inc(g.shld, 16)
                    if a:
                        wait(sp, g.xc, t, 32, 0, s_bog)
                        wait(sp, g.a_free, t, NA, -NA)
                        load_batch(t, par)
                    if c:
                        bc = t.before(2)
                        wait(sp, g.os, bc, GROUPS, GROUPS, s_bog)
                        wait(sp, g.on, bc, 1, 1)
                        sp.dma_start(zl[:, :], osum[par][DK::2 * DK, :, :]).then_inc(g.zl, 16)
                        for half in range(2):
                            for j in range(GH):
                                if (half, j) == (1, 0):
                                    wait(sp, g.rz, bc, 1, 1)
                                    sp.dma_start(z_dram.rearrange("j g t -> (j g t)").rearrange("(p n) -> p n", p=P),
                                                 zr[:, :]).then_inc(g.zst, 16)
                                dst0 = 64 * half + DK * j
                                src = osum[par][2 * DK * j:2 * DK * j + DK, half::2, :]
                                sp.dma_start(oc[dst0:dst0 + DK, :, :], src).then_inc(g.oz, 16)
                        wait(sp, g.zst, bc, 16, 16)
                        for half in range(2):
                            for j in range(GH):
                                dst0 = 64 * half + DK * j
                                src = z_dram[j:j + 1, half::2, :].to_broadcast([DK, CT, T])
                                sp.dma_start(zc[dst0:dst0 + DK, :, :], src).then_inc(g.oz, 16)
                    if a:
                        wait(sp, g.qk, t, 16 * 4 * PARTS, 0, s_bog)
                        wait(sp, g.kl, t, 1, 1)
                        sp.dma_start(k_dram.rearrange("h (m p) t -> p h m t", p=P), ks[:, :, :, :]).then_inc(g.qkst, 16)
                        wait(sp, g.ql, t, 1, 1)
                        sp.dma_start(q_dram.rearrange("h (m p) t -> p h m t", p=P), qs[:, :, :, :]).then_inc(g.qkst, 16)
                        wait(sp, g.qkst, t, 32, 32, s_bog)
                        wait(sp, g.full, t, 2 * VS, -2 * VS)
                        sp.wait_ge(s_rows[par], 4)
                        for s in range(2):
                            for r, (qp, kp) in enumerate(((0, 0), (1, 0), (0, 1))):
                                for stack, dram, part in ((Q, q_dram, qp), (K, k_dram, kp)):
                                    src = dram[part].rearrange("(g s c) t -> s c g t", s=2, c=DK)[s]
                                    sp.dma_start(stack[par][64 * s + DK * r:64 * s + DK * (r + 1), :, :], src)\
                                        .then_inc(g.qk, 16)
                    if c:
                        bc = t.before(2)
                        wait(sp, g.c_free, bc, NCU, C_USES["o1"] + 2, s_bog)
                        sp.dma_start(out_v[bass.ds(bc.value(), 1)].rearrange("b p m t -> p (b m) t"),
                                     res[:, bass.ds(bc.value(CT * T), CT * T)].rearrange("p (m t) -> p m t", m=CT))\
                            .then_inc(g.outst, 16)
                        wait(sp, g.x2l, bc, 1, 1, s_bog)
                        dst = xn_dram[bass.ds(bc.value(C), C)].rearrange("(m p) (h t) -> p h m t", p=P, h=2)
                        sp.dma_start(dst, xs2[:, :, :, :]).then_inc(g.xnst, 16)

                slots(sp, slot)
                sp.wait_ge(g.xnst, 16 * B + 16)
                sp.wait_ge(g.outst, 16 * B)

            both_runs(sp, attention)

            sp.sem_inc(s_stored, 1)
            sp.wait_ge(s_pool_c, 5)
            for n in range(TT):
                sp.dma_start(out[TOK:TOK + P, n * P:(n + 1) * P], ones[:, :]).then_inc(s_spare, 16)
            for n in range(2):
                sp.wait_ge(s_wst[n], 16 * 2 * (NE - 1))
            for e in range(EB // 2, NE):
                if e == EB:
                    sp.wait_ge(s_table, 2)
                if e >= EB:
                    end = sp.value_load(table[0:1, TILES + e - EB:TILES + e - EB + 1], min_val=1,
                                        max_val=TILES + 1)
                    sp.wait_ge(s_y, end)
                if e == NE - 1:
                    for n in range(2):
                        sp.wait_ge(s_wst[n], 16 * 2 * NE)
                sp.wait_ge(s_wr, 16 * e)
                sp.dma_start(W[:, (e % EB) * 2 * WCOL:(e % EB + 1) * 2 * WCOL],
                             w_dram[e].rearrange("p h n -> p (h n)")).then_inc(s_wr, 16)
            sp.wait_ge(s_wr, 16 * NE)

        @block.gpsimd
        def _(pool):
            pool.memset(ident[:, :], 0.0).then_inc(s_pool_c, 1)
            pool.memset(ones[:, :], 1.0).then_inc(s_pool_c, 1)
            pool.memset(neg_half[:, :], -0.5).then_inc(s_pool_c, 1)
            pool.wait_ge(s_pool_c, 3)
            pool.affine_select(out=ident[:, :], in_=ident[:, :], compare_op=ALU.not_equal, fill=1.0, base=0,
                               pattern=[[-1, P]], channel_multiplier=1).then_inc(s_pool_c, 1)
            pool.affine_select(out=below[:, :], in_=ones[:, :], compare_op=ALU.is_gt, fill=0.0, base=0,
                               pattern=[[1, P]], channel_multiplier=-1).then_inc(s_pool_c, 1)
            pool.wait_ge(s_pool_c, 5)
            pool.tensor_copy(ident16[:, :], ident[:, :]).then_inc(s_vone, 1)
            for i in range(2):
                pool.memset(V[i][:, :, :, DK:2 * DK], 1.0).then_inc(s_vone, 1)
            pool.iota(iota_i[:, :], pattern=[[1, P]], base=0, channel_multiplier=0).then_inc(s_num, 1)
            pool.iota(tok_i[:, :], pattern=[[0, TOP], [P, NT]], base=0, channel_multiplier=1).then_inc(s_num, 1)
            pool.memset(keep_et[:, :], 1.0).then_inc(s_num, 1)
            pool.wait_ge(s_num, 3)
            pool.tensor_copy(iota_f[:, :], iota_i[:, :]).then_inc(s_num, 1)
            pool.tensor_copy(tok_f[:, :], tok_i[:, :]).then_inc(s_num, 1)
            pool.memset(keep_et[:, ::NT], 0.0).then_inc(s_num, 1)

            def attention(pool, g, guard):
                def lo_part(b, parts, f, hi, lo):
                    wait(pool, hi, b, 1, 1)
                    pool.tensor_tensor(parts[:, 1], f[:, :, :], parts[:, 0], ALU.subtract).then_inc(lo, 1)

                def slot(pool, t, par, a, b_, c):
                    if a:
                        pool.wait_ge(s_pool_c, 5)
                        lo_part(t, cs, ctx_sb[par], g.ch, g.cl)
                        wait(pool, g.mv, t, CT, CT, s_pool_c)
                        pool.tensor_scalar(veps[:, :], mv[:, :, 1], EPS, None, ALU.add).then_inc(g.veps, 1)
                        wait(pool, g.veps, t, 1, 1)
                        pool.tensor_tensor(rstd[:, :], veps[:, :], neg_half[:, :], ALU.pow).then_inc(g.rstd, 1)
                        lo_part(t, xs, xn, g.xh, g.xl)
                        lo_part(t, ks, kf, g.kh, g.kl)
                    if c:
                        lo_part(t.before(2), os_, on, g.oh, g.ol)
                    if a:
                        lo_part(t, qs, qf, g.qh, g.ql)
                    if c:
                        bc = t.before(2)
                        wait(pool, g.mv2, bc, CT, CT, s_pool_c)
                        pool.tensor_scalar(veps2[:, :], mv2[:, :, 1], EPS, None, ALU.add).then_inc(g.veps2, 1)
                        wait(pool, g.veps2, bc, 1, 1)
                        pool.tensor_tensor(rstd2[:, :], veps2[:, :], neg_half[:, :], ALU.pow).then_inc(g.rstd2, 1)
                        wait(pool, g.x2h, bc, 1, 1)
                        pool.tensor_tensor(xs2[:, 1], xn2[:, :, :], xs2[:, 0], ALU.subtract).then_inc(g.x2l, 1)

                slots(pool, slot)

            both_runs(pool, attention)

            pool.wait_ge(s_hot, 1)
            for n, values in enumerate((w_hi, w_lo)):
                pool.tensor_tensor(til_w[:, :, n, :], til_tok[:, :, 0, :],
                                   values[:, :].unsqueeze(2).to_broadcast([P, TOP * NT, TILES]), ALU.mult)\
                    .then_inc(s_tilw, 1)

            pool.wait_ge(s_tok, 1)
            def gather(j):
                if j >= TR:
                    pool.wait_ge(s_xt, j - TR + 1)
                pool.indirect_dma_start(out=xg[j % TR][:, :], out_offset=None, in_=xn_dram[:, :],
                                        in_offset=bass.IndirectOffsetOnAxis(ap=slot_tok[:, j:j + 1], axis=0))\
                    .then_inc(s_xg[j % TR], 16)

            for j in range(TR):
                gather(j)
            pool.wait_ge(s_tok, 2)
            pool.wait_ge(s_spare, 16 * TT)
            pool.wait_ge(s_stored, 1)
            for j in range(TILES):
                pool.wait_ge(s_yo, j + 1)
                if j >= 1:
                    pool.wait_ge(s_add, 16 * j)
                pool.indirect_dma_start(out=out[:, :],
                                        out_offset=bass.IndirectOffsetOnAxis(ap=slot_out[:, j:j + 1], axis=0),
                                        in_=yo[j % TR][:, :], in_offset=None, compute_op=ALU.add)\
                    .then_inc(s_add, 16)
                if j + TR < TILES:
                    gather(j + TR)
            pool.wait_ge(s_add, 16 * TILES)

        @block.scalar
        def _(act):
            act.dma_start(bv_r, bv.rearrange("(a n) -> a n", a=1)).then_inc(s_rowc, 16)
            for n, g_ in enumerate((g_xattn, g_ffn)):
                act.dma_start(g_r[:, n:n + 1], g_.rearrange("(a n) -> a n", a=1)).then_inc(s_rowc, 16)
            for dst, src in ((bq_c, bq), (bk_c, bk), (bo_c, bo)):
                act.dma_start(dst, src).then_inc(s_const2, 16)
            for n, src in enumerate((WqT, WvT, WoT)):
                act.dma_start(w4[:, n + 1, :, :], src.rearrange("(k p) n -> p k n", p=P)).then_inc(s_const2, 16)
            act.dma_start(gate[:, :, :], gateT.rearrange("(k p) n -> p k n", p=P)).then_inc(s_const2, 16)
            act.wait_ge(s_bias, 2)
            act.activation(tg_c, cols[:, 4 * CT + 2:4 * CT + 4], ACT.Tanh).then_inc(s_tanh, 1)

            def shift_rows(stacks, factor):
                for r0 in (64 * s + 32 for s in range(2)):
                    act.activation(stacks[0][r0:r0 + 32, :, :].rearrange("p g t -> p (g t)"),
                                   ones[r0:r0 + 32, 0:1].to_broadcast([32, G * T]), ACT.Copy, scale=factor)\
                        .then_inc(s_rows[0], 1)

            def load_quarter(e, c):
                act.dma_start(wf[c % 2][:, :], wall[bass.ds(e.value(), 1), :, c * WQ:(c + 1) * WQ]
                              .rearrange("e p n -> p (e n)")).then_inc(s_wf[c % 2], 16)

            def store_quarter(e, c):
                wait(act, s_wlo, e, 4, c + 1, s_bias)
                act.dma_start(w_dram[bass.ds(e.value(), 1), :, :, c * WQ:(c + 1) * WQ]
                              .rearrange("e p h n -> p (e h) n"), wp[c % 2][:, :, :]).then_inc(s_wst[c % 2], 16)
                e, c = (e, c + 2) if c < 2 else (e.before(-1), c - 2)
                if e.i is not None or e.add < NE:
                    load_quarter(e, c)

            def attention(act, g, guard):
                if not guard:
                    act.wait_ge(g.xc, 32)
                    for n in range(2):
                        load_quarter(At(None, 0, 0), n)
                    shift_rows(K, SHIFT)
                    shift_rows(Q, 0.0)

                def slot(act, t, par, a, b_, c):
                    splits = [] if guard else quarters(t)
                    if not b_:
                        for _, e, c in splits:
                            store_quarter(e, c)
                        return
                    b = t.before(1)
                    for u in range(2 * VS):
                        wait(act, g.full, b, 2 * VS, u + 1)
                        wait(act, g.pv, b, VS, u // 2 - RING // 2 + 1)
                        act.activation(prob[:, u % RING, :], S[u % 2][:, :], ACT.Exp, scale=SCALE).then_inc(g.exp, 1)
                        for v, e, c in splits:
                            if u == 2 * min(v + 2, VS - 1) + 1:
                                store_quarter(e, c)

                slots(act, slot)
                act.wait_ge(g.pv, B * VS)
                act.wait_ge(g.oz, OZ * B + 16)

            both_runs(act, attention)

            for n in range(2):
                act.wait_ge(s_wst[n], 16 * 2 * (NE - 1))
            for e in range(EB // 2):
                if e >= 1:
                    act.wait_ge(s_wr, 16 * e)
                act.dma_start(W[:, e * 2 * WCOL:(e + 1) * 2 * WCOL], w_dram[e].rearrange("p h n -> p (h n)"))\
                    .then_inc(s_wr, 16)
            act.wait_ge(s_wexp, 1)
            act.activation(el[:, :], dl[:, :], ACT.Exp).then_inc(s_wexp, 1)
            act.activation(warm[:, :], ones[:, 0:1], ACT.Silu)

            def gate_tile(act, j, n):
                wait(act, s_h1, j, 1, 1)
                if n >= 2:
                    wait(act, s_hh, j, 1, -1)
                act.activation(act1[n % 2][:, :], h1_ps, ACT.Silu, scale=1.0 / WS).then_inc(s_silu, 1)

            def hi_part(act, j, n):
                wait(act, s_hh, j, 1, 1)
                if n >= 2:
                    wait(act, s_ht, j, 1, -1)
                act.activation(hs[n % 2][:, 0:F], hh[n % 2][:, :], ACT.Copy).then_inc(s_hi, 1)

            def weigh(act, j, n):
                wait(act, s_y, j, 1, 2)
                if n >= TR:
                    wait(act, s_add, j, 16, 16 - 16 * TR)
                act.activation(yo[n % TR][:, :], y_ps[:, :], ACT.Copy, scale=slot_w[:, bass.ds(j.value(), 1)])\
                    .then_inc(s_yo, 1)

            def step(act, j, n):
                gate_tile(act, j, n)
                hi_part(act, j, n)
                if n >= 1:
                    weigh(act, j.before(1), n - 1)
                if j.i is None and 1 <= j.add <= 2:
                    store_quarter(At(None, 0, NE - 1), j.add + 1)

            act.wait_ge(s_tok, 3)
            tiles(act, step)
            weigh(act, At(None, 0, TILES - 1), TILES - 1)

        @block.vector
        def _(dve):
            def split_projections(ns):
                for n in ns:
                    dve.tensor_scalar(w4s[:, 0, n], w4[:, n], WS, None, ALU.mult).then_inc(s_w4, 1)
                    dve.wait_ge(s_w4, 2 * n + 1)
                    dve.scalar_tensor_tensor(out=w4s[:, 1, n], in0=w4[:, n], scalar=WS, in1=w4s[:, 0, n],
                                             op0=ALU.mult, op1=ALU.subtract).then_inc(s_w4, 1)

            dve.wait_ge(s_const, 16)
            split_projections((0,))
            dve.wait_ge(s_init, 1)
            dve.tensor_copy(bv_all[:, :], MA[:, 0:C]).then_inc(s_bias, 1)
            dve.tensor_copy(cols[:, 4 * CT + 2:4 * CT + 4], MA[:, C:C + 2]).then_inc(s_bias, 1)

            steps = [0]

            def done(ins):
                steps[0] += 1
                ins.then_inc(s_r, 1)
                return steps[0]

            def then(n):
                dve.wait_ge(s_r, n)

            def best(sem_best, n0, n1):
                for n in range(n0, n1):
                    dve.max(top8[:, n, :], logits[:, n * NE:(n + 1) * NE]).then_inc(sem_best, 1)
                dve.wait_ge(sem_best, n1 - n0)
                for n in range(n0, n1):
                    dve.max_index(idx8[:, n, :], top8[:, n, :], logits[:, n * NE:(n + 1) * NE]).then_inc(sem_best, 1)
                dve.wait_ge(sem_best, 2 * (n1 - n0))

            def split_quarter(e, c):
                wait(dve, s_wf[c % 2], e, 16 * 2, 16 * (c // 2 + 1), s_tanh)
                wait(dve, s_wst[c % 2], e, 16 * 2, 16 * (c // 2), s_tanh)
                dve.tensor_scalar(wp[c % 2][:, 0], wf[c % 2][:, :], WS, None, ALU.mult).then_inc(s_whi, 1)
                wait(dve, s_whi, e, 4, c + 1)
                dve.scalar_tensor_tensor(out=wp[c % 2][:, 1], in0=wf[c % 2][:, :], scalar=WS,
                                         in1=wp[c % 2][:, 0], op0=ALU.mult, op1=ALU.subtract).then_inc(s_wlo, 1)

            def attention(dve, g, guard):
                dve.sem_inc(g.c_free, 1)
                dve.sem_inc(g.on, 1)
                dve.sem_inc(g.ol, 1)
                if not guard:
                    dve.memset(ok[:, :], 1.0).then_inc(g.ok, 1)

                def rest(b, m, n=1):
                    return res[:, bass.ds(b.value(CT * T, m * T), n * T)]

                def slot(dve, t, par, a, b_, c):
                    bb, bc = t.before(1), t.before(2)
                    if b_ and guard:
                        wait(dve, g.turned, bb, 1)
                        for u in range(UM):
                            wait(dve, g.raw, bb, UM, u + 1)
                            dve.tensor_reduce(maxima[:, 2 * u:2 * u + 2],
                                              S[u % 2][:, :].rearrange("p (n t) -> p n t", n=2), AX_X, ALU.max)\
                                .then_inc(g.top, 1)
                        wait(dve, g.turned, bb, 1, 1)
                        wait(dve, g.shst, bb, 16)
                        dve.tensor_scalar(shift_t[:, :], O[0][0:H * TT, 0:P], -1.0 / SHIFT, None, ALU.mult)\
                            .then_inc(g.shift, 1)
                    if c:
                        for m in range(CT):
                            dve.tensor_scalar(rest(bc, m), rest(bc, m), bog_c[:, m:m + 1], None, ALU.add)\
                                .then_inc(g.xb, 1)
                    splits = [] if guard else quarters(t)
                    for v, e, n in splits:
                        if v == 0:
                            split_quarter(e, n)
                    if c:
                        wait(dve, g.zl, bc, 16, 16)
                        if not guard:
                            for n, (bound, op) in enumerate(((Z_LEAST, ALU.is_ge), (Z_MOST, ALU.is_le))):
                                wait(dve, g.ok, bc, 2, 1 + n)
                                dve.scalar_tensor_tensor(out=ok[:, :], in0=zl[:, :], scalar=bound,
                                                         in1=ok[:, :], op0=op, op1=ALU.mult).then_inc(g.ok, 1)
                        dve.reciprocal(zr[:, :], zl[:, :]).then_inc(g.rz, 1)
                        if not (a or b_) and not guard:
                            dve.wait_ge(g.ok, 2 * B + 1)
                            dve.tensor_reduce(ok_min[:, :], ok[:, :], AX_X, ALU.min).then_inc(s_okall, 1)
                            dve.wait_ge(s_oksum, 1)
                            dve.tensor_scalar(bad[:, :], MC[:, 0:1], P - 0.5, None, ALU.is_lt).then_inc(s_bad, 1)
                        if not (a or b_):
                            dve.wait_ge(g.c_free, NCU * (B - 1) + 1)
                            best(g.best, 0, NT - CT)
                    if a:
                        wait(dve, g.xc, t, 32, 32, s_tanh)
                        wait(dve, g.a_full, t, NA)
                        dve.tensor_copy(cs[:, 0], ctx_sb[par][:, :, :]).then_inc(g.ch, 1)
                        for m in range(CT):
                            dve.bn_stats(stats[:, m, :], rest(t, m)).then_inc(g.bst, 1)
                        for m in range(CT):
                            wait(dve, g.bst, t, CT, m + 1, s_tanh)
                            dve.bn_aggr(mv[:, m, :], stats[:, m, :]).then_inc(g.mv, 1)
                    for v in range(VS):
                        what = EXTRA.get(v)
                        if t.i is None and t.add == 0 and not guard and v == VS - 1:
                            for r0 in (64 * s + 32 for s in range(2)):
                                dve.memset(Q[1][r0:r0 + 32, :, :], 0.0).then_inc(s_rows[1], 1)
                                dve.memset(K[1][r0:r0 + 32, :, :], SHIFT).then_inc(s_rows[1], 1)
                        if t.i is None and t.add == 0 and not guard and v == SPLIT_AT:
                            split_projections((2, 3))
                            dve.wait_ge(s_tanh, 1)
                            dve.tensor_scalar(bog_c, bo_c, tg_c[:, 0:1], None, ALU.mult).then_inc(s_bog, 1)
                            dve.tensor_scalar(tgs_c, tg_c[:, 0:1], 1.0 / WS, None, ALU.mult).then_inc(s_bog, 1)
                            dve.wait_ge(s_bog, 2)
                        if t.i is None and t.add == 0 and not guard and v == 2:
                            dve.wait_ge(s_const2, 16 * NCONST2)
                            split_projections((1,))
                        if a and v == 2:
                            wait(dve, g.rstd, t, 1, 1)
                            wait(dve, g.xl, t, 1)
                            for m in range(CT):
                                dve.tensor_scalar(xn[:, m, :], rest(t, m), mv[:, m, 0:1], rstd[:, m:m + 1],
                                                  ALU.subtract, ALU.mult).then_inc(g.xn, 1)
                            wait(dve, g.xn, t, CT, CT)
                            dve.tensor_copy(xs[:, 0], xn[:, :, :]).then_inc(g.xh, 1)
                        if c and v == ON_AT:
                            wait(dve, g.oz, bc, OZ, OZ + 16)
                            wait(dve, g.ol, bc, 1, 1)
                            if a:
                                wait(dve, g.kl, t, 1, 1)
                            dve.tensor_tensor(on[:, :, :], oc[:, :, :], zc[:, :, :], ALU.mult).then_inc(g.on, 1)
                            wait(dve, g.on, bc, 1, 2)
                            dve.tensor_copy(os_[:, 0], on[:, :, :]).then_inc(g.oh, 1)
                        if a and what in A_USES:
                            wait(dve, g.a_full, t, NA, A_USES[what] + 1)
                            m = int(what[1])
                            if what[0] in "qk":
                                f, bias, lo = (qf, bq_c, g.ql) if what[0] == "q" else (kf, bk_c, g.kl)
                                wait(dve, lo, t, 1)
                                if what == "k0":
                                    wait(dve, g.ol, t, 1, -1)
                                dve.tensor_scalar(f[:, m, :], MA[:, :], 1.0 / WS, bias[:, m:m + 1], ALU.mult, ALU.add)\
                                    .then_inc(g.a_free, 1)
                                if m == CT - 1:
                                    parts, hi = (qs, g.qh) if what[0] == "q" else (ks, g.kh)
                                    wait(dve, g.qkst, t, 32)
                                    wait(dve, g.a_free, t, NA, A_USES[what] + 1)
                                    dve.tensor_copy(parts[:, 0], f[:, :, :]).then_inc(hi, 1)
                            else:
                                if m == 0:
                                    wait(dve, g.pv, t, VS, -VS)
                                for i in range(2):
                                    last = dve.scalar_tensor_tensor(
                                        out=V[par][:, 2 * m + i, :, 0:DK],
                                        in0=MA[:, i * C:(i + 1) * C].rearrange("p (h c) -> p h c", h=H),
                                        scalar=1.0 / WS, in1=bv_all[:, :].rearrange("p (h c) -> p h c", h=H),
                                        op0=ALU.mult, op1=ALU.add)
                                last.then_inc(g.a_free, 1)
                        if c and what in C_USES:
                            wait(dve, g.c_full, bc, NCU, C_USES[what] + 1)
                            if what[0] == "o":
                                m = int(what[1])
                                wait(dve, g.xb, bc, CT, m + 1)
                                dve.scalar_tensor_tensor(out=rest(bc, m), in0=MC[:, :], scalar=tgs_c,
                                                         in1=rest(bc, m), op0=ALU.mult, op1=ALU.add).then_inc(g.c_free, 1)
                            elif what[0] == "t":
                                dve.tensor_copy(xT2[:, int(what[1]), :], MC[:, :]).then_inc(g.c_free, 1)
                            elif what == "lg":
                                dve.tensor_copy(lgT[:, :], MC[0:NE, 0:C]).then_inc(g.c_free, 1)
                            else:
                                dve.tensor_copy(logits[:, bass.ds(bc.value(CT * NE), CT * NE)], MC[:, 0:CT * NE])\
                                    .then_inc(g.c_free, 1)
                            if what == "o1":
                                for m in range(CT):
                                    wait(dve, g.c_free, bc, NCU, m + 2, s_tanh)
                                    dve.bn_stats(stats2[:, m, :], rest(bc, m)).then_inc(g.bst2, 1)
                                for m in range(CT):
                                    wait(dve, g.bst2, bc, CT, m + 1, s_tanh)
                                    dve.bn_aggr(mv2[:, m, :], stats2[:, m, :]).then_inc(g.mv2, 1)
                        if c and v == XN2_AT:
                            wait(dve, g.rstd2, bc, 1, 1)
                            wait(dve, g.xnst, bc, 16, 16)
                            for m in range(CT):
                                dve.tensor_scalar(xn2[:, m, :], rest(bc, m), mv2[:, m, 0:1], rstd2[:, m:m + 1],
                                                  ALU.subtract, ALU.mult).then_inc(g.xn2, 1)
                            wait(dve, g.xn2, bc, CT, CT)
                            dve.tensor_copy(xs2[:, 0], xn2[:, :, :]).then_inc(g.x2h, 1)
                        if b_ and v % TT == TT - 1:
                            g4 = v // TT
                            wait(dve, g.pv, bb, VS, v + 1)
                            wait(dve, g.oz, bb, OZ, 16 - OZ)
                            dve.tensor_copy(osum[1 - par][:, g4, :], O[g4 % 2][:, :]).then_inc(g.os, 1)
                        for at, e, n in splits:
                            if at == v > 0:
                                split_quarter(e, n)

                slots(dve, slot)
                dve.wait_ge(g.xnst, 16 * B + 16)
                dve.wait_ge(g.c_free, NCU * B + 1)

            both_runs(dve, attention)

            dve.sem_inc(s_done, 1)
            dve.wait_ge(s_done, 2)
            best(s_best, NT - CT, NT)
            dve.tensor_tensor(dl[:, :], top8[:, :, 1], top8[:, :, 0], ALU.subtract).then_inc(s_wexp, 1)
            last = done(dve.tensor_copy(idxf[:, :, :], idx8[:, :, 0:TOP].rearrange("p n k -> p k n")))
            then(last)
            dve.wait_ge(s_num, 6)
            e_row = iota_f[:, 0:NE].unsqueeze(1).to_broadcast([P, NT, NE])
            for k in range(TOP):
                last = done(dve.tensor_tensor(onehot[:, k], e_row, idxf[:, k].unsqueeze(2).to_broadcast([P, NT, NE]),
                                              ALU.is_equal))
            then(last)
            ranks[0] = done(dve.tensor_tensor(picks[:, :, :], onehot[:, 0], onehot[:, 1], ALU.add))
            dve.wait_ge(s_wexp, 2)
            last = done(dve.tensor_scalar(el1[:, :], el[:, :], 1.0, None, ALU.add))
            then(last)
            last = done(dve.reciprocal(cw[:, 0], el1[:, :]))
            then(last)
            last = done(dve.tensor_tensor(cw[:, 1], cw[:, 0], el[:, :], ALU.mult))
            then(last)
            last = done(dve.tensor_scalar(cwg[:, :, :], cw[:, :, :], tg_c[:, 1:2], None, ALU.mult))
            then(last)
            last = done(dve.tensor_copy(w_hi[:, :], cwg[:, :, :].rearrange("p k n -> p (k n)")))
            then(last)
            last = done(dve.tensor_tensor(w_rest[:, :], cwg[:, :, :].rearrange("p k n -> p (k n)"), w_hi[:, :],
                                          ALU.subtract))
            then(last)
            last = done(dve.tensor_scalar(w_lo[:, :], w_rest[:, :], LO, None, ALU.mult))
            for n, sign in enumerate((-1.0, 1.0)):
                last = done(dve.tensor_scalar(spare[:, n:n + 1], tok_f[:, 0:1], float(TOK), sign, ALU.add, ALU.mult))
            dve.wait_ge(s_rank, 1)
            last = done(dve.tensor_copy(count_et[:, :].rearrange("p (e n) -> p e n", e=NE),
                                        MC[:, 0:NT * NE].rearrange("p (n e) -> p e n", e=NE)))
            then(last)
            last = done(dve.tensor_tensor_scan(upto_et[:, :], keep_et[:, :], count_et[:, :], 0.0, ALU.mult, ALU.add))
            then(last)
            last = done(dve.tensor_tensor(prev_et[:, :], upto_et[:, :], count_et[:, :], ALU.subtract))
            last = done(dve.tensor_scalar(tot_f[:, :], upto_et[:, NT - 1::NT], float(P - 1), None, ALU.add))
            then(last)
            last = done(dve.tensor_copy(tot_i[:, :], tot_f[:, :]))
            then(last)
            last = done(dve.tensor_scalar(ntl_i[:, :], tot_i[:, :], 7, None, ALU.logical_shift_right))
            then(last)
            last = done(dve.tensor_copy(ntl[:, :], ntl_i[:, :]))
            then(last)
            last = done(dve.tensor_tensor_scan(endt[:, :], ones[:, 0:NE], ntl[:, :], 0.0, ALU.mult, ALU.add))
            then(last)
            last = done(dve.tensor_tensor(startt[:, :], endt[:, :], ntl[:, :], ALU.subtract))
            then(last)
            last = done(dve.scalar_tensor_tensor(
                out=prev_et[:, :].rearrange("p (e n) -> p e n", e=NE),
                in0=startt[:, :].unsqueeze(2).to_broadcast([P, NE, NT]), scalar=float(P),
                in1=prev_et[:, :].rearrange("p (e n) -> p e n", e=NE), op0=ALU.mult, op1=ALU.add))
            then(last)
            last = done(dve.tensor_tensor(slot_e[:, :, :], MA[:, 0:NT * NE].rearrange("p (n e) -> p n e", e=NE),
                                          prev_et[:, :].rearrange("p (e n) -> p n e", e=NE), ALU.add))
            then(last)
            for k in range(TOP):
                last = done(dve.tensor_tensor(slot_m[:, k], onehot[:, k], slot_e[:, :, :], ALU.mult))
            then(last)
            last = done(dve.tensor_reduce(slot_f[:, :], slot_m[:, :, :, :].rearrange("p k n e -> p (k n) e"), AX_X,
                                          ALU.add))
            then(last)
            last = done(dve.tensor_copy(slot_i[:, :], slot_f[:, :]))
            then(last)
            last = done(dve.tensor_scalar(til_i[:, :], slot_i[:, :], 7, None, ALU.logical_shift_right))
            last = done(dve.tensor_scalar(row_i[:, :], slot_i[:, :], P - 1, None, ALU.bitwise_and))
            then(last)
            last = done(dve.tensor_copy(til_f[:, :], til_i[:, :]))
            last = done(dve.tensor_copy(row_f[:, :], row_i[:, :]))
            then(last)
            PAIRS = TOP * NT
            last = done(dve.tensor_tensor(til_tok[:, :, 0, :], iota_f[:, 0:TILES].unsqueeze(1).to_broadcast([P, PAIRS, TILES]),
                                          til_f[:, :].unsqueeze(2).to_broadcast([P, PAIRS, TILES]), ALU.is_equal))
            then(last)
            dve.sem_inc(s_hot, 1)
            last = done(dve.tensor_tensor(til_tok[:, :, 1, :], til_tok[:, :, 0, :],
                                          tok_f[:, :].unsqueeze(2).to_broadcast([P, PAIRS, TILES]), ALU.mult))
            for n in range(0, PAIRS, HOT):
                hots.append(done(dve.tensor_tensor(
                    row_hot[:, n:n + HOT, :], iota_f[:, :].unsqueeze(1).to_broadcast([P, HOT, P]),
                    row_f[:, n:n + HOT].unsqueeze(2).to_broadcast([P, HOT, P]), ALU.is_equal)))
            dve.wait_ge(s_tab, 1)
            tab = MC[:, 0:2 * TILES].rearrange("p (k n) -> p k n", k=2)
            dve.tensor_copy(slot_tok[:, :], tab[:, 1]).then_inc(s_tok, 1)
            last = done(dve.tensor_scalar(slot_pad[:, :], tab[:, 0], spare[:, 0:1], spare[:, 1:2], ALU.mult, ALU.add))
            then(last)
            dve.tensor_tensor(slot_out[:, :], tab[:, 1], slot_pad[:, :], ALU.add).then_inc(s_tok, 1)
            last = done(dve.tensor_tensor(le[:, :, :], endt[:, :].unsqueeze(1).to_broadcast([P, TILES, NE]),
                                          iota_f[:, 0:TILES].unsqueeze(2).to_broadcast([P, TILES, NE]), ALU.is_le))
            then(last)
            last = done(dve.tensor_reduce(et_f[:, :], le[:, :, :], AX_X, ALU.add))
            then(last)
            last = done(dve.tensor_scalar(et_f[:, :], et_f[:, :], float(NE - 1), None, ALU.min))
            then(last)
            dve.tensor_scalar(table[:, TILES:TILES + NE], endt[:, :], 1.0, None, ALU.add).then_inc(s_table, 1)
            dve.tensor_scalar(table[:, 0:TILES], et_f[:, :], 1.0, 16.0, ALU.add, ALU.mult).then_inc(s_table, 1)
            dve.wait_ge(s_tab, 2)
            last = done(dve.tensor_scalar(slot_w[:, :], MA[:, TILES:2 * TILES], 1.0 / (LO * WS * HS), None, ALU.mult))
            then(last)
            dve.scalar_tensor_tensor(out=slot_w[:, :], in0=MA[:, 0:TILES], scalar=1.0 / (WS * HS), in1=slot_w[:, :],
                                     op0=ALU.mult, op1=ALU.add).then_inc(s_tok, 1)

            def x_out(dve, j, n):
                wait(dve, s_xt, j, 1, 1)
                if n >= 2:
                    wait(dve, s_h, j, 1, -1)
                dve.tensor_copy(xT[n % 2][:, :, :], xt_ps.rearrange("p (k n) -> p k n", n=P)).then_inc(s_xT, 1)

            def step(dve, j, n):
                par = n % 2
                wait(dve, s_silu, j, 1, 1)
                if n >= 1:
                    wait(dve, s_ht, j, 1, -1)
                wait(dve, s_h, j, 1, 1)
                dve.scalar_tensor_tensor(out=hh[par][:, :], in0=h3_ps, scalar=HS / WS, in1=act1[par][:, :],
                                         op0=ALU.mult, op1=ALU.mult).then_inc(s_hh, 1)
                if n < TILES - 1:
                    x_out(dve, At(j.i, j.mul, j.add + 1), n + 1)
                wait(dve, s_hi, j, 1, 1)
                dve.tensor_tensor(hs[par][:, F:F + FL], hh[par][:, F - FL:F], hs[par][:, F - FL:F], ALU.subtract)
                dve.tensor_tensor(hs[par][:, F + FL:2 * F], hh[par][:, 0:F - FL], hs[par][:, 0:F - FL], ALU.subtract)\
                    .then_inc(s_lo, 1)
                wait(dve, s_ht, j, 1, 1)
                if n >= 2:
                    wait(dve, s_y, j, 1)
                dve.tensor_copy(hT[par][:, :, :], ht_ps[:, 0:HB * P].rearrange("p (k n) -> p k n", n=P))\
                    .then_inc(s_hT, 1)

                if j.i is None and j.add < 2:
                    split_quarter(At(None, 0, NE - 1), j.add + 2)

            x_out(dve, At(None, 0, 0), 0)
            tiles(dve, step)

        @block.tensor
        def _(pe):
            pe.wait_ge(s_rowc, 16 * 3)
            pe.wait_ge(s_pool_c, 5)
            pe.matmul(MA[:, 0:C], ones[0:1, :], bv_r, start=True, stop=True)
            pe.matmul(MA[:, C:C + 2], ones[0:1, :], g_r, start=True, stop=True).then_inc(s_init, 1)
            pe.wait_ge(s_bias, 2)

            def attention(pe, g, guard):
                def scores(b, par, v):
                    g4, st = divmod(v, TT)
                    if v == 0:
                        wait(pe, g.qk, b, 16 * 4 * PARTS, 16 * 4 * PARTS)
                    for n in range(2):
                        u = 2 * v + n
                        wait(pe, g.exp, b, 2 * VS, u - 1)
                        for s in range(2):
                            r0 = 64 * s
                            last = pe.matmul(S[u % 2][:, s * T:(s + 1) * T],
                                             K[par][r0:r0 + PARTS * DK + 1, 2 * g4 + n, st * P:(st + 1) * P],
                                             Q[par][r0:r0 + PARTS * DK + 1, 2 * g4 + n, :], start=True, stop=True)
                        last.then_inc(g.full, 1)

                def row_maxima(b, par):
                    wait(pe, g.qk, b, 16 * 4 * PARTS, 16 * 4 * PARTS)
                    wait(pe, g.exp, b, 2 * VS)
                    for u in range(UM):
                        h = u // (TT // 2)
                        r0 = 64 * (h % 2)
                        wait(pe, g.top, b, UM, u - 1)
                        for n in range(2):
                            tt = 2 * (u % (TT // 2)) + n
                            last = pe.matmul(S[u % 2][:, n * T:(n + 1) * T],
                                             Q[par][r0:r0 + PARTS * DK, h // 2, tt * P:(tt + 1) * P],
                                             K[par][r0:r0 + PARTS * DK, h // 2, :], start=True, stop=True)
                        last.then_inc(g.raw, 1)
                    wait(pe, g.top, b, UM, UM)
                    wait(pe, g.os, b, GROUPS, 0, s_bias)
                    pe.transpose(O[0][0:H * TT, 0:P], maxima[:, :], ident[:, :]).then_inc(g.turned, 1)
                    wait(pe, g.shld, b, 32, 32)

                def values(b, par, v):
                    g4, st = divmod(v, TT)
                    if v == 0:
                        wait(pe, g.a_free, b, NA, A_USES["v1"] + 1)
                        pe.wait_ge(s_vone, 3)
                    wait(pe, g.exp, b, 2 * VS, 2 * v + 2)
                    if st == 0:
                        wait(pe, g.os, b, GROUPS, g4 - 1)
                    for j in range(GH):
                        u = 2 * v + j // 2
                        last = pe.matmul(O[g4 % 2][2 * DK * j:2 * DK * (j + 1), :], V[par][:, st, GH * g4 + j, :],
                                         prob[:, u % RING, (j % 2) * T:(j % 2 + 1) * T],
                                         start=(st == 0), stop=(st == TT - 1), tile_position=(0, 2 * DK * j))
                    last.then_inc(g.pv, 1)

                PASSES = ((0, 0), (1, 0), (0, 1))

                def project(t, par, what):
                    m = int(what[1])
                    if t.i is None and t.add == 0:
                        pe.wait_ge(s_w4, {"k": 2, "q": 4, "v": 6}[what[0]])
                    wait(pe, g.a_free, t, NA, A_USES[what])
                    if what[0] == "v":
                        for i in range(2):
                            st = 2 * m + i
                            for n, (wp_, xp) in enumerate(PASSES):
                                for k in range(CT):
                                    last = pe.matmul(MA[:, i * C:(i + 1) * C], cs[:, xp, k, st * P:(st + 1) * P],
                                                     w4s[:, wp_, 2, k, :], start=(n == 0 and k == 0),
                                                     stop=(n == len(PASSES) - 1 and k == CT - 1))
                    else:
                        w, src, hi, lo = (1, xs, g.xh, g.xl) if what[0] == "q" else (0, cs, g.ch, g.cl)
                        last = three(MA, w, m, src, t, hi, lo, m == 0, 1)
                    last.then_inc(g.a_full, 1)

                def three(bank, w, m, src, b, hi, lo, first, c):
                    for n, (wp_, xp) in enumerate(PASSES):
                        if first and n == 0:
                            if w == 3 and b.i is not None:
                                pe.wait_ge(s_w4, 8)
                            wait(pe, hi, b, 1, 1)
                        if first and xp == 1:
                            wait(pe, lo, b, 1, c)
                        for k in range(CT):
                            last = pe.matmul(bank[:, :], w4s[:, wp_, w, k, m * P:(m + 1) * P], src[:, xp, k, :],
                                             start=(n == 0 and k == 0), stop=(n == len(PASSES) - 1 and k == CT - 1))
                    return last

                def output(b, what):
                    wait(pe, g.c_free, b, NCU, C_USES[what] + 1, s_bias if what == "lt" else None)
                    if what[0] == "o":
                        m = int(what[1])
                        last = three(MC, 3, m, os_, b, g.oh, g.ol, m == 0, 2)
                    elif what[0] == "t":
                        m = int(what[1])
                        wait(pe, g.xn2, b, CT, m + 1)
                        for k in range(TT):
                            last = pe.transpose(MC[:, k * P:(k + 1) * P], xn2[:, m, k * P:(k + 1) * P], ident[:, :])
                    elif what == "lt":
                        for m in range(CT):
                            last = pe.transpose(MC[:, m * NE:(m + 1) * NE], lgT[:, m * P:(m + 1) * P],
                                                ident[0:NE, 0:NE])
                    else:
                        for k in range(TT):
                            last = pe.matmul(MC[0:NE, 0:C], gate[:, k, :], xT2[:, :, k * P:(k + 1) * P],
                                             start=(k == 0), stop=(k == TT - 1))
                    last.then_inc(g.c_full, 1)

                def slot(pe, t, par, a, b_, c):
                    bb, bc = t.before(1), t.before(2)
                    first = t.i is None and t.add == 1
                    last_b = t.i is None and t.add == B
                    if b_ and guard:
                        row_maxima(bb, 1 - par)
                    if b_ and (first or guard):
                        scores(bb, 1 - par, 0)
                    if not (a or b_) and not guard:
                        pe.wait_ge(g.c_free, NCU * (B - 1) + 1)
                        pe.wait_ge(s_okall, 1)
                        pe.matmul(MC[:, 0:1], ones[:, :], ok_min[:, :], start=True, stop=True).then_inc(s_oksum, 1)
                        pe.wait_ge(s_bad, 1)
                    for v in range(VS):
                        if b_ and v + 1 < VS:
                            scores(bb, 1 - par, v + 1)
                        what = EXTRA.get(v)
                        if a and what in A_USES:
                            project(t, par, what)
                        if c and what in C_USES:
                            output(bc, what)
                        if b_:
                            if v == VS - 1 and not last_b and not guard:
                                scores(t, par, 0)
                            values(bb, 1 - par, v)

                slots(pe, slot)
                pe.wait_ge(g.c_free, NCU * B + 1)

            both_runs(pe, attention)

            pe.sem_inc(s_done, 1)
            pe.wait_ge(s_r, ranks[0])
            pe.matmul(MA[:, 0:NT * NE], below[:, :], picks[:, :, :].rearrange("p n e -> p (n e)"), start=True, stop=True)
            pe.matmul(MC[:, 0:NT * NE], ones[:, :], picks[:, :, :].rearrange("p n e -> p (n e)"), start=True, stop=True)\
                .then_inc(s_rank, 1)
            for n in range(TOP * NT):
                if n % HOT == 0:
                    pe.wait_ge(s_r, hots[n // HOT])
                last = pe.matmul(MC[:, 0:2 * TILES], row_hot[:, n, :], til_tok[:, n, :, :].rearrange("p k n -> p (k n)"),
                                 start=(n == 0), stop=(n == TOP * NT - 1))
            last.then_inc(s_tab, 1)
            pe.wait_ge(s_tilw, 2)
            for n in range(TOP * NT):
                last = pe.matmul(MA[:, 0:2 * TILES], row_hot[:, n, :], til_w[:, n, :, :].rearrange("p k n -> p (k n)"),
                                 start=(n == 0), stop=(n == TOP * NT - 1))
            last.then_inc(s_tab, 1)
            pe.wait_ge(s_table, 2)
            pe.sem_inc(s_y, 1)

            def turn_x(j, n):
                pe.wait_ge(s_xg[n % TR], At(j.i, j.mul // TR, j.add // TR).value(16, 16))
                wait(pe, s_xT, j, 1)
                for k in range(2 * TT):
                    last = pe.transpose(xt_ps[:, k * P:(k + 1) * P], xg[n % TR][:, k * P:(k + 1) * P], ident16[:, :])
                last.then_inc(s_xt, 1)

            def weights_of(j):
                landed = pe.value_load(table[0:1, bass.ds(j.value(), 1)], min_val=16, max_val=16 * NE)
                return landed, ((landed - 16) & (16 * (EB - 1))) * (2 * WCOL // 16)

            def hidden(j, par, off):
                for n, (ps, full) in enumerate(((h1_ps, s_h1), (h3_ps, s_h))):
                    for k in range(TT):
                        for xp, w in ((0, 0), (0, 1), (1, 0)):
                            last = pe.matmul(ps, xT[par][:, xp * TT + k, :],
                                             W[:, bass.ds(off + (w * WCOL + (2 * k + n) * F), F)],
                                             start=(k == 0 and (xp, w) == (0, 0)),
                                             stop=(k == TT - 1 and (xp, w) == (1, 0)))
                    last.then_inc(full, 1)

            def turn_h(j, par):
                wait(pe, s_lo, j, 1, 1)
                wait(pe, s_hT, j, 1)
                for k in range(HB):
                    c = (F + FL if k % 2 else 0) + k // 2 * P if k < HB - 1 else F - FL
                    last = pe.transpose(ht_ps[:, k * P:(k + 1) * P], hs[par][:, c:c + P], ident16[:, :])
                last.then_inc(s_ht, 1)

            def down(j, par, off):
                wait(pe, s_hT, j, 1, 1)
                wait(pe, s_yo, j, 1)
                products = [(2 * k + hp, P, k, w) for k in range(FT - 1) for hp, w in ((0, 0), (0, 1), (1, 0))]
                products += [(HB - 1, FL, FT - 1, 1), (HB - 1, P, FT - 1, 0)]
                for n, (block, rows_, k, w) in enumerate(products):
                    last = pe.matmul(y_ps[:, :], hT[par][0:rows_, block, :],
                                     W[0:rows_, bass.ds(off + (w * WCOL + W2 + k * T), T)],
                                     start=(n == 0), stop=(n == len(products) - 1))
                last.then_inc(s_y, 1)

            def step(pe, j, n):
                if n >= 1:
                    _, off_before = weights_of(j.before(1))
                landed, off = weights_of(j)
                pe.wait_ge(s_wr, landed)
                wait(pe, s_xT, j, 1, 1)
                if n >= 1:
                    turn_h(j.before(1), (n - 1) % 2)
                hidden(j, n % 2, off)
                if n < TILES - 1:
                    turn_x(At(j.i, j.mul, j.add + 1), n + 1)
                if n >= 1:
                    down(j.before(1), (n - 1) % 2, off_before)

            turn_x(At(None, 0, 0), 0)
            tiles(pe, step)
            turn_h(At(None, 0, TILES - 1), (TILES - 1) % 2)
            down(At(None, 0, TILES - 1), (TILES - 1) % 2, weights_of(At(None, 0, TILES - 1))[1])


def kernel(**inputs):
    import numpy as np
    import concourse.bacc as bacc
    from concourse.bass_utils import run_bass_kernel_spmd

    a = {k: np.asarray(v) for k, v in inputs.items()}
    w1, w3, w2 = a["L0_ffn_w1"], a["L0_ffn_w3"], a["L0_ffn_w2"]
    NE, F, T = w1.shape
    FT = -(-F // P)
    w13 = np.concatenate([w1, w3], axis=1).transpose(0, 2, 1).reshape(NE, T // P, P, 2 * F)
    w2T = np.zeros((NE, FT * P, T), w2.dtype)
    w2T[:, :F] = w2.transpose(0, 2, 1)
    w2T[:, F:] = w2T[:, 2 * F - FT * P:F]
    wall = np.concatenate([w13.transpose(0, 2, 1, 3).reshape(NE, P, -1),
                           w2T.reshape(NE, FT, P, T).transpose(0, 2, 1, 3).reshape(NE, P, -1)], axis=2)
    arrays = {
        "x": a["x"], "ctx_in": a["ctx_2048"], "g_xattn": a["g_xattn"], "g_ffn": a["g_ffn"],
        "WqT": a["L0_xattn_Wq"].T, "bq": a["L0_xattn_bq"], "WkT": a["L0_xattn_Wk"].T, "bk": a["L0_xattn_bk"],
        "WvT": a["L0_xattn_Wv"].T, "bv": a["L0_xattn_bv"], "WoT": a["L0_xattn_Wo"].T, "bo": a["L0_xattn_bo"],
        "gateT": a["L0_ffn_gate_w"].T,
        "wall": wall,
    }
    for k in ("bq", "bk", "bo"):
        arrays[k] = arrays[k].reshape(-1, P).T
    arrays = {k: np.ascontiguousarray(v) for k, v in arrays.items()}
    nc = bacc.Bacc("TRN2", target_bir_lowering=False, num_devices=1)
    args = [nc.dram_tensor(k, v.shape, mybir.dt.from_np(v.dtype), kind="ExternalInput").ap()
            for k, v in arrays.items()]
    B, C, T = a["x"].shape
    out = nc.dram_tensor("out", [B * C + P, T], F32, kind="ExternalOutput").ap()
    flamingo_kernel(nc, *args, out)
    r = run_bass_kernel_spmd(nc, [arrays], core_ids=[0])
    return r.results[0]["out"][:B * C].reshape(B, C, T)
```
